# Optimizing a Trainium2 kernel written in Bass

```python
import numpy as np
import jax
import jax.numpy as jnp

def _softmax(x, axis=-1):
    return jax.nn.softmax(x, axis=axis)

def _gelu(x):
    return jax.nn.gelu(x, approximate=True)

def _silu(x):
    return jax.nn.silu(x)

def _sigmoid(x):
    return jax.nn.sigmoid(x)

def _layernorm(x, axis=-1, eps=1e-05):
    m = jnp.mean(x, axis=axis, keepdims=True)
    v = jnp.var(x, axis=axis, keepdims=True)
    return (x - m) / jnp.sqrt(v + eps)

def _scatter_add(tgt, idx, src, axis=0):
    return tgt.at[idx].add(src)

def _segment_sum(src, seg, n):
    return jax.ops.segment_sum(src, seg, n)
kernel_name = 'mk_xattn_ffn_d1_seqx_r4_89987b'

def setup_inputs(seed: int=0):
    np.random.seed(seed)
    _w = jnp.asarray

    def _rec_inputs():
        import jax
        import jax.numpy as jnp
        _rk = jax.random.key(seed)
        x = -0.0002928 + 1 * jax.random.normal(jax.random.fold_in(_rk, 1), (8, 512, 256), jnp.float32)
        _lenS = 512 - jax.random.randint(jax.random.fold_in(_rk, 7), (8,), 0, max(1, 512 // 4) + 1, jnp.int32)
        _lenS2 = 64 - jax.random.randint(jax.random.fold_in(_rk, 8), (8,), 0, max(1, 64 // 4) + 1, jnp.int32)
        _ctx_512P = jax.random.normal(jax.random.fold_in(_rk, 11), (8, 16, 128), jnp.float32)
        _ctx_512c = jax.random.dirichlet(jax.random.fold_in(_rk, 511), 0.3 * jnp.ones((16,), jnp.float32), (8, 64))
        _ctx_512t = jnp.einsum('bsk,bkd->bsd', _ctx_512c, _ctx_512P)
        _ctx_512t = _ctx_512t * jax.lax.rsqrt(jnp.mean(jnp.square(_ctx_512t)) + 1e-12) * 0.953939
        ctx_512 = 0.00222621 + 0.99962 * (_ctx_512t + 0.3 * jax.random.normal(jax.random.fold_in(_rk, 611), (8, 64, 128), jnp.float32))
        return (x, ctx_512)
    x, ctx_512 = _rec_inputs()

    def _L0_xattn_setup():
        import jax, jax.numpy as jnp
        import numpy as np
        B, T, TC, C, CC, H = (2, 512, 128, 256, 128, 16)
        D = C // H

        def _heads(t):
            b, l, _ = t.shape
            return t.reshape(b, l, H, D).transpose(0, 2, 1, 3)
        key = jax.random.key(seed)
        ks = jax.random.split(key, 18)
        w = lambda k, i, o: jax.random.normal(k, (i, o), jnp.float32) / np.sqrt(i).astype(np.float32)
        return {'x': jax.random.normal(ks[0], (B, T, C), jnp.float32), 'cross_input': jax.random.normal(ks[1], (B, TC, CC), jnp.float32), 'Wk': w(ks[2], C, C), 'bk': jnp.zeros((C,), jnp.float32), 'Wq': w(ks[3], C, C), 'bq': jnp.zeros((C,), jnp.float32), 'Wv': w(ks[4], C, C), 'bv': jnp.zeros((C,), jnp.float32), 'Wck': w(ks[5], CC, C), 'bck': jnp.zeros((C,), jnp.float32), 'Wcq': w(ks[6], C, C), 'bcq': jnp.zeros((C,), jnp.float32), 'Wcv': w(ks[7], CC, C), 'bcv': jnp.zeros((C,), jnp.float32), 'Wp': w(ks[8], C, C), 'bp': jnp.zeros((C,), jnp.float32)}
    _L0_xattn_all = _L0_xattn_setup()
    _L0_xattn_in = {k: v for k, v in _L0_xattn_all.items() if k in ('Wk', 'bk', 'Wq', 'bq', 'Wv', 'bv', 'Wck', 'bck', 'Wcq', 'bcq', 'Wcv', 'bcv', 'Wp', 'bp')}
    del _L0_xattn_all

    def _L0_ffn_setup():
        import jax, jax.numpy as jnp
        import numpy as np
        D = 256
        H = 1024
        E = 64
        K = 3
        B, S = (2, 512)
        C = 128
        key = jax.random.key(seed)
        ks = jax.random.split(key, 6)
        s = 0.02
        return {'x': jax.random.normal(ks[0], (B, S, D), jnp.float32), 'gate_w': jax.random.normal(ks[1], (D, E), jnp.float32) * s, 'gate_b': jnp.zeros((E,), jnp.float32), 'w1': jax.random.normal(ks[2], (E, D, H), jnp.float32) * s, 'b1': jnp.zeros((E, H), jnp.float32), 'w2': jax.random.normal(ks[3], (E, H, D), jnp.float32) * s, 'b2': jnp.zeros((E, D), jnp.float32)}
    _L0_ffn_all = _L0_ffn_setup()
    _L0_ffn_in = {k: v for k, v in _L0_ffn_all.items() if k in ('gate_w', 'gate_b', 'w1', 'b1', 'w2', 'b2')}
    del _L0_ffn_all
    return {'x': x, 'ctx_512': ctx_512, 'L0_xattn_Wk': _L0_xattn_in['Wk'], 'L0_xattn_bk': _L0_xattn_in['bk'], 'L0_xattn_Wq': _L0_xattn_in['Wq'], 'L0_xattn_bq': _L0_xattn_in['bq'], 'L0_xattn_Wv': _L0_xattn_in['Wv'], 'L0_xattn_bv': _L0_xattn_in['bv'], 'L0_xattn_Wck': _L0_xattn_in['Wck'], 'L0_xattn_bck': _L0_xattn_in['bck'], 'L0_xattn_Wcq': _L0_xattn_in['Wcq'], 'L0_xattn_bcq': _L0_xattn_in['bcq'], 'L0_xattn_Wcv': _L0_xattn_in['Wcv'], 'L0_xattn_bcv': _L0_xattn_in['bcv'], 'L0_xattn_Wp': _L0_xattn_in['Wp'], 'L0_xattn_bp': _L0_xattn_in['bp'], 'L0_ffn_gate_w': _L0_ffn_in['gate_w'], 'L0_ffn_gate_b': _L0_ffn_in['gate_b'], 'L0_ffn_w1': _L0_ffn_in['w1'], 'L0_ffn_b1': _L0_ffn_in['b1'], 'L0_ffn_w2': _L0_ffn_in['w2'], 'L0_ffn_b2': _L0_ffn_in['b2']}

def reference(x, ctx_512, L0_xattn_Wk, L0_xattn_bk, L0_xattn_Wq, L0_xattn_bq, L0_xattn_Wv, L0_xattn_bv, L0_xattn_Wck, L0_xattn_bck, L0_xattn_Wcq, L0_xattn_bcq, L0_xattn_Wcv, L0_xattn_bcv, L0_xattn_Wp, L0_xattn_bp, L0_ffn_gate_w, L0_ffn_gate_b, L0_ffn_w1, L0_ffn_b1, L0_ffn_w2, L0_ffn_b2):
    import jax
    import jax.numpy as jnp

    def _L0_xattn_ref(x, cross_input, Wk, bk, Wq, bq, Wv, bv, Wck, bck, Wcq, bcq, Wcv, bcv, Wp, bp):
        import jax, jax.numpy as jnp
        import numpy as np
        B, T, TC, C, CC, H = (2, 512, 128, 256, 128, 16)
        D = C // H

        def _heads(t):
            b, l, _ = t.shape
            return t.reshape(b, l, H, D).transpose(0, 2, 1, 3)
        scale = np.float32(1.0 / np.sqrt(D))
        q = _heads(x @ Wq + bq)
        k = _heads(x @ Wk + bk)
        v = _heads(x @ Wv + bv)
        att = jnp.einsum('bhqd,bhkd->bhqk', q, k) * scale
        causal = jnp.tril(jnp.ones((T, T), bool))
        att = jnp.where(causal[None, None], att, -jnp.inf)
        y = jnp.einsum('bhqk,bhkd->bhqd', jax.nn.softmax(att, axis=-1), v)
        qc = _heads(x @ Wcq + bcq)
        kc = _heads(cross_input @ Wck + bck)
        vc = _heads(cross_input @ Wcv + bcv)
        attc = jnp.einsum('bhqd,bhkd->bhqk', qc, kc) * scale
        y = y + jnp.einsum('bhqk,bhkd->bhqd', jax.nn.softmax(attc, axis=-1), vc)
        y = y.transpose(0, 2, 1, 3).reshape(x.shape[0], T, C)
        return y @ Wp + bp

    def _L0_ffn_ref(x, gate_w, gate_b, w1, b1, w2, b2):
        import jax, jax.numpy as jnp
        import numpy as np
        D = 256
        H = 1024
        E = 64
        K = 3
        B, S = (2, 512)
        C = 128
        xf = x.reshape(-1, D)
        T = xf.shape[0]
        logits = xf @ gate_w + gate_b
        top_l, top_i = jax.lax.top_k(logits, K)
        gates = jax.nn.softmax(top_l, axis=-1)
        fe = top_i.reshape(-1)
        fg = gates.reshape(-1)
        tok = jnp.repeat(jnp.arange(T), K)
        oh = jax.nn.one_hot(fe, E, dtype=jnp.int32)
        pos = (jnp.cumsum(oh, axis=0) * oh).sum(-1) - 1
        valid = pos < C
        buf = jnp.zeros((E, C, D), x.dtype).at[fe, pos].set(xf[tok], mode='drop')
        h = jax.nn.gelu(jnp.einsum('ecd,edh->ech', buf, w1) + b1[:, None, :], approximate=False)
        y = jnp.einsum('ech,ehd->ecd', h, w2) + b2[:, None, :]
        rows = y[fe, jnp.minimum(pos, C - 1)] * (fg * valid.astype(x.dtype))[:, None]
        out = jnp.zeros_like(xf).at[tok].add(rows)
        return out.reshape(x.shape)
    x = x + _L0_xattn_ref(_layernorm(x, axis=-1), ctx_512, L0_xattn_Wk, L0_xattn_bk, L0_xattn_Wq, L0_xattn_bq, L0_xattn_Wv, L0_xattn_bv, L0_xattn_Wck, L0_xattn_bck, L0_xattn_Wcq, L0_xattn_bcq, L0_xattn_Wcv, L0_xattn_bcv, L0_xattn_Wp, L0_xattn_bp)
    x = x + _L0_ffn_ref(_layernorm(x, axis=-1), L0_ffn_gate_w, L0_ffn_gate_b, L0_ffn_w1, L0_ffn_b1, L0_ffn_w2, L0_ffn_b2)
    return x

_drawn_inputs = setup_inputs


def setup_inputs(seed=0):
    import zlib

    import numpy as np

    out = dict(_drawn_inputs(seed))
    spreads = {'L0_xattn_bk': (0.0, 0.8),
     'L0_xattn_bq': (0.0, 0.488),
     'L0_xattn_bv': (0.0, 0.1),
     'L0_xattn_bck': (0.0, 0.8),
     'L0_xattn_bcq': (0.0, 0.304),
     'L0_xattn_bcv': (0.0, 0.1),
     'L0_xattn_bp': (0.0, 0.1),
     'L0_ffn_gate_b': (0.0, 0.1),
     'L0_ffn_b1': (0.0, 0.609),
     'L0_ffn_b2': (0.0, 0.1)}
    factors = {}
    for name, (base, spread) in spreads.items():
        noise = np.random.default_rng([zlib.crc32(name.encode()), seed]).standard_normal(out[name].shape)
        drawn = base * np.exp(spread * noise) if base else spread * noise
        out[name] = jnp.asarray(drawn.astype(out[name].dtype))
    for name, factor in factors.items():
        out[name] = (out[name] * factor).astype(out[name].dtype)
    return out
```

```python
from contextlib import ExitStack

import concourse.bass as bass
from concourse import mybir

ALU = mybir.AluOpType
ACT = mybir.ActivationFunctionType
AX = mybir.AxisListType
F32 = mybir.dt.float32
BF16 = mybir.dt.bfloat16
I32 = mybir.dt.int32
U32 = mybir.dt.uint32

P = 128
B, S, C = 8, 512, 256
CC, SC = 128, 64
H, D = 16, 16
G = 4
U = H // G
NT = S // P
KC = C // P
N = B * S
E, TOPK, CAP, F = 64, 3, 128, 1024
FC = F // P
EPS = 1e-5
PARTS = 3
QPARTS = (0, 1, 2, 0, 1, 0)
KPARTS = (0, 0, 0, 1, 1, 2)
KQ = len(KPARTS) * D
KM = KQ + PARTS
HD = 32
WID = [S - P * j for j in range(NT)]
OFF = [sum(WID[:j]) for j in range(NT)]
PW = sum(WID)
NA, NB = 13, 7
SCALE = D ** -0.5
LOW = -1e30


def wait(eng, sem, value):
    if not isinstance(value, int) or value > 0:
        eng.wait_ge(sem, value)


def wait_apart(pool, sem, value, passed):
    wait(pool, sem, value)
    pool.sem_inc(passed, 1)


class At:

    def __init__(self, b, u, total):
        self.b, self.u, self.total = b, u, total
        self.s = b * U + u + 1
        self.exists = not isinstance(self.s, int) or 1 <= self.s <= total

    def back(self, k):
        if isinstance(self.b, int):
            s = self.s - k - 1
            return At(s // U, s % U, self.total)
        carry = (self.u - k) // U
        return At(self.b + carry, (self.u - k) % U, self.total)

    def uses(self, ring, each):
        return (self.s - 1 - self.u % ring) * (each // ring)


def steps(eng, total, extra, body):
    for s in range(2 * U):
        body(At(s // U, s % U, total))
    with eng.Fori(2, total // U - 1, 1) as b:
        for u in range(U):
            body(At(b, u, total))
    for s in range(total - U, total + extra):
        body(At(s // U, s % U, total))


def layer_kernel(nc, x, ctx, Wk, bk, Wq, bq, Wv, bv, Wck, bck, Wcq, bcq, Wcv, bcv, Wp, bp,
                 gate_w, gate_b, w1, b1, w2, b2, out):
    def dram(name, shape, dt):
        return nc.dram_tensor(name, shape, dt).ap()

    q_d = dram("q_parts", [B, PARTS * D, 2, H * S], BF16)
    k_d = dram("k_parts", [B, PARTS * D, 1, H * S], BF16)
    ck_d = dram("ck_parts", [PARTS * D, H, B * SC], BF16)
    v_d = dram("v_rows", [B, S, H * HD], F32)
    cv_d = dram("cv_rows", [B * SC, H * HD], F32)
    y_d = dram("attention", [B, U, S, G * D], F32)
    xn_d = dram("xn_rows", [N + P, C], F32)
    tab_d = dram("slot_table", [CAP * E, 2], I32)
    b2_d = dram("b2_parts", [PARTS, E, C], BF16)

    with ExitStack() as whole:
        ps = whole.enter_context(nc.psum_tensor("ps", [P, 8, 512], F32))
        ident = whole.enter_context(nc.sbuf_tensor("ident", [P, P], F32))
        identb = whole.enter_context(nc.sbuf_tensor("identb", [P, P], BF16))
        w1_sb = whole.enter_context(nc.sbuf_tensor("w1_sb", [P, U, KC, F], F32))
        w2_sb = whole.enter_context(nc.sbuf_tensor("w2_sb", [P, U, FC, C], F32))
        w_in = [whole.enter_context(nc.semaphore(f"w_in{r}")) for r in range(U)]

        project(nc, ps, ident, identb, x, ctx, Wk, bk, Wq, bq, Wv, bv, Wck, bck, Wcq, bcq, Wcv, bcv,
                q_d, k_d, ck_d, v_d, cv_d, xn_d, tab_d, out)
        attend(nc, ps, ident, identb, q_d, k_d, ck_d, v_d, cv_d, y_d)
        route(nc, ps, ident, x, Wp, bp, gate_w, gate_b, w1, w2, b2, y_d, xn_d, tab_d, b2_d, out,
              w1_sb, w2_sb, w_in)
        experts(nc, ps, ident, w1, b1, w2, xn_d, tab_d, b2_d, out, w1_sb, w2_sb, w_in)


def load_expert(eng, w1, w2, w1_sb, w2_sb, w_in, e, ring):
    eng.dma_start(w1_sb[:, ring], w1[bass.ds(e, 1)].rearrange("e (c p) f -> p (e c) f", p=P)).then_inc(w_in[ring], 16)
    eng.dma_start(w2_sb[:, ring], w2[bass.ds(e, 1)].rearrange("e (c p) d -> p (e c) d", p=P)).then_inc(w_in[ring], 16)


def project(nc, ps, ident, identb, x, ctx, Wk, bk, Wq, bq, Wv, bv, Wck, bck, Wcq, bcq, Wcv, bcv,
            q_d, k_d, ck_d, v_d, cv_d, xn_d, tab_d, out):
    NCH = 3 * KC
    with ExitStack() as st:
        def sb(name, shape, dt):
            return st.enter_context(nc.sbuf_tensor(name, shape, dt))

        def sem(name):
            return st.enter_context(nc.semaphore("p_" + name))

        wq_sb, wk_sb, wcq_sb, wv_sb = (sb(n, [P, KC, C], F32) for n in ("wq_sb", "wk_sb", "wcq_sb", "wv_sb"))
        wck_sb, wcv_sb = (sb(n, [P, C], F32) for n in ("wck_sb", "wcv_sb"))
        bias = sb("bias", [P, 4, KC], F32)
        scaled = sb("scaled", [P, 4, KC], F32)
        bv_sb, bcv_sb = (sb(n, [P, C], F32) for n in ("bv_sb", "bcv_sb"))
        x_sb = sb("x_sb", [P, 2, NT, C], F32)
        xn_sb = sb("xn_sb", [P, 2, NT, C], F32)
        xT = sb("xT", [P, 2, KC, S], F32)
        cx = sb("cx", [P, NT, CC], F32)
        cxT = sb("cxT", [P, S], F32)
        stats = sb("stats", [P, NT, 6], F32)
        mv = sb("mv", [P, NT, 2], F32)
        base = sb("base", [P, NT], F32)
        rstd = sb("rstd", [P, NT], F32)
        power = sb("power", [P, NT], F32)
        full = sb("full", [P, 2, S], F32)
        rest = sb("rest", [P, 2, S], F32)
        parts = sb("parts", [P, 2, PARTS, S], BF16)
        va = sb("va", [P, 2, H, HD], F32)
        zero = sb("zero", [P, C], F32)
        ids = sb("ids", [P, E, 2], I32)

        consts, w_ready, c_in = sem("consts"), sem("w_ready"), sem("c_in")
        x_in = [sem("x_in0"), sem("x_in1")]
        bias_ready, var_ready, rstd_ready, xn_ready = (sem(n) for n in ("bias", "var", "rstd", "xn"))
        cT_psum, cT_ready, xT_psum, xT_ready = (sem(n) for n in ("cT_psum", "cT_ready", "xT_psum", "xT_ready"))
        chunk_psum, full_ready, parts_ready = (sem(n) for n in ("chunk_psum", "full", "parts"))
        parts_out = [sem("parts_out0"), sem("parts_out1")]
        v_psum, v_ready = sem("v_psum"), sem("v_ready")
        v_out = [sem("v_out0"), sem("v_out1")]
        init_out, passed = sem("init_out"), sem("passed")
        weights = [(wq_sb, 0, q_d, 0), (wk_sb, 1, k_d, 0), (wcq_sb, 2, q_d, 1)]
        LOADS = 12
        blk = st.enter_context(nc.Block())

        def chunk(b, n):
            return KC + NCH * b + n

        def tile(b, t):
            return NT + NT * b + t

        def batches(eng, body):
            for u in range(2):
                body(u, u, False)
            with eng.Fori(1, B // 2 - 1, 1) as i:
                for u in range(2):
                    body(i * 2 + u, u, False)
            for u in range(2):
                body(B - 2 + u, u, u == 1)

        @blk.sync
        def _(sp):
            def load_x(b, u):
                wait(sp, xn_ready, b - 1)
                sp.dma_start(x_sb[:, u], x[bass.ds(b, 1)].rearrange("b (t p) c -> p (b t) c", p=P)).then_inc(x_in[u], 16)

            def store_parts(g, par, dst):
                sp.wait_ge(parts_ready, g + 1)
                for i in range(PARTS):
                    sp.dma_start(dst(i), parts[:, par, i, :]).then_inc(parts_out[par], 16)

            def store_values(g, par, dst, src):
                sp.wait_ge(v_ready, g + 1)
                sp.dma_start(dst, src).then_inc(v_out[par], 16)

            load_x(0, 0)
            for w, d in ((Wck, wck_sb), (Wcv, wcv_sb)):
                sp.dma_start(d[:], w).then_inc(w_ready, 16)
            for w, d in ((Wq, wq_sb), (Wk, wk_sb), (Wcq, wcq_sb), (Wv, wv_sb)):
                sp.dma_start(d[:], w.rearrange("(c p) n -> p c n", p=P)).then_inc(w_ready, 16)
            with nc.allow_non_contiguous_dma(reason="biases by channel"):
                for i, b_ in enumerate((bq, bk, bcq, bck)):
                    sp.dma_start(bias[:, i, :], b_.rearrange("(c p) -> p c", p=P)).then_inc(w_ready, 16)
            for b_, d in ((bv, bv_sb), (bcv, bcv_sb)):
                sp.dma_start(d[:], b_.rearrange("(a c) -> a c", a=1).to_broadcast([P, C])).then_inc(w_ready, 16)
            load_x(1, 1)
            for g in range(KC):
                store_parts(g, g, lambda i: ck_d[i * D:(i + 1) * D, g * (H // KC):(g + 1) * (H // KC), :].rearrange("d h n -> h d n"))
            for t in range(NT):
                store_values(t, t % 2, cv_d[t * P:(t + 1) * P, :], va[:, t % 2].rearrange("p h f -> p (h f)"))

            def batch(b, u, last):
                for n in range(NCH):
                    (dst, which), oc = weights[n // KC][2:], n % KC
                    rows = dst[bass.ds(b, 1), :, which, oc * (H // KC) * S:(oc + 1) * (H // KC) * S]
                    store_parts(chunk(b, n), n % 2, lambda i: rows[:, i * D:(i + 1) * D].rearrange("b d (h n) -> (b h) d n", n=S))
                    if n == 3 and not (last or (isinstance(b, int) and b >= B - 2)):
                        load_x(b + 2, u)
                for t in range(NT):
                    store_values(tile(b, t), t % 2, v_d[bass.ds(b, 1), t * P:(t + 1) * P, :].rearrange("b t f -> (b t) f"),
                                 va[:, t % 2].rearrange("p h f -> p (h f)"))

            batches(sp, batch)
            for par in range(2):
                sp.wait_ge(parts_out[par], 16 * PARTS * (chunk(B, 0) // 2))
                sp.wait_ge(v_out[par], 16 * (tile(B, 0) // 2))

        @blk.gpsimd
        def _(pool):
            pool.memset(ident[:], 0.0)
            pool.memset(power[:], -0.5)
            pool.memset(zero[:], 0.0)
            pool.memset(va[:], 1.0)
            pool.memset(ids[:], 0)
            pool.drain()
            pool.affine_select(out=ident[:], in_=ident[:], compare_op=ALU.not_equal, fill=1.0, base=0,
                               pattern=[[-1, P]], channel_multiplier=1)
            pool.iota(ids[:, :, 0], pattern=[[0, E]], base=N, channel_multiplier=1)
            pool.drain()
            pool.tensor_copy(identb[:], ident[:]).then_inc(consts, 1)
            pool.wait_ge(consts, 1)
            pool.dma_start(xn_d[N:N + P, :], zero[:]).then_inc(init_out, 16)
            pool.dma_start(out[N:N + P, :], zero[:]).then_inc(init_out, 16)
            pool.dma_start(tab_d.rearrange("(p e) t -> p (e t)", p=P), ids[:].rearrange("p e t -> p (e t)")).then_inc(init_out, 16)
            with pool.Fori(0, B, 1) as b:
                wait_apart(pool, var_ready, b + 1, passed)
                pool.tensor_scalar(base[:], mv[:, :, 1], EPS, None, ALU.add)
                pool.drain()
                pool.tensor_tensor(rstd[:], base[:], power[:], ALU.pow).then_inc(rstd_ready, 1)
            pool.wait_ge(init_out, 48)

        @blk.tensor
        def _(pe):
            def transposes(b, u):
                pe.wait_ge(xn_ready, b + 1)
                wait(pe, xT_ready, b)
                for c in range(KC):
                    for t in range(NT):
                        mm = pe.transpose(ps[:, c, t * P:(t + 1) * P], xn_sb[:, u, t, c * P:(c + 1) * P], ident[:])
                mm.then_inc(xT_psum, 1)

            pe.wait_ge(consts, 1)
            pe.wait_ge(c_in, 16)
            for t in range(NT):
                mm = pe.transpose(ps[:, 6, t * P:(t + 1) * P], cx[:, t, :], ident[:])
            mm.then_inc(cT_psum, 1)
            transposes(0, 0)
            pe.wait_ge(cT_ready, 1)
            pe.wait_ge(w_ready, 16 * LOADS)
            for oc in range(KC):
                pe.matmul(ps[:, 2 + oc, :], wck_sb[:, oc * P:(oc + 1) * P], cxT[:], start=True, stop=True).then_inc(chunk_psum, 1)
            for t in range(NT):
                wait(pe, v_ready, t - 1)
                pe.matmul(ps[:, 6 + t % 2, 0:C], cxT[:, t * P:(t + 1) * P], wcv_sb[:], start=True, stop=True).then_inc(v_psum, 1)

            def batch(b, u, last):
                pe.wait_ge(xT_ready, b + 1)
                for n in range(NCH):
                    w, oc = weights[n // KC][0], n % KC
                    g = chunk(b, n)
                    bank = 2 + chunk(u, n) % 4
                    wait(pe, full_ready, g - 3)
                    for c in range(KC):
                        mm = pe.matmul(ps[:, bank, :], w[:, c, oc * P:(oc + 1) * P], xT[:, u, c, :],
                                       start=(c == 0), stop=(c == KC - 1))
                    mm.then_inc(chunk_psum, 1)
                    if n == 3 and not last:
                        transposes(b + 1, 1 - u)
                for t in range(NT):
                    wait(pe, v_ready, tile(b, t) - 1)
                    for c in range(KC):
                        mm = pe.matmul(ps[:, 6 + t % 2, 0:C], xT[:, u, c, t * P:(t + 1) * P], wv_sb[:, c, :],
                                       start=(c == 0), stop=(c == KC - 1))
                    mm.then_inc(v_psum, 1)

            batches(pe, batch)

        @blk.scalar
        def _(act):
            def copy_x(b, u):
                act.wait_ge(xT_psum, b + 1)
                wait(act, v_psum, tile(b, 0) - NT)
                act.copy(xT[:, u, 0, :], ps[:, 0, :])
                act.copy(xT[:, u, 1, :], ps[:, 1, :]).then_inc(xT_ready, 1)

            def copy_chunk(g, par, bank, kind, oc):
                act.wait_ge(chunk_psum, g + 1)
                wait(act, parts_ready, g - 1)
                wait(act, parts_out[par], 8 * PARTS * (g - par))
                scale = SCALE if kind in (0, 2) else 1.0
                act.activation(parts[:, par, 0], ps[:, bank, :], ACT.Identity, bias=scaled[:, kind, oc:oc + 1], scale=scale)
                act.activation(full[:, par], ps[:, bank, :], ACT.Identity, bias=scaled[:, kind, oc:oc + 1],
                               scale=scale).then_inc(full_ready, 1)

            act.dma_start(cx[:], ctx.rearrange("b k c -> (b k) c").rearrange("(t p) c -> p t c", p=P)).then_inc(c_in, 16)
            act.wait_ge(cT_psum, 1)
            act.copy(cxT[:], ps[:, 6, :]).then_inc(cT_ready, 1)
            copy_x(0, 0)
            act.wait_ge(bias_ready, 1)
            for g in range(KC):
                copy_chunk(g, g, 2 + g, 3, g)

            def batch(b, u, last):
                for n in range(NCH):
                    copy_chunk(chunk(b, n), n % 2, 2 + chunk(u, n) % 4, weights[n // KC][1], n % KC)
                    if n == 3 and not last:
                        copy_x(b + 1, 1 - u)

            batches(act, batch)

        @blk.vector
        def _(dve):
            def normalise(b, u):
                dve.wait_ge(x_in[u], 8 * (b - u) + 16)
                for t in range(NT):
                    dve.bn_stats(stats[:, t], x_sb[:, u, t])
                dve.drain()
                for t in range(NT):
                    mean = dve.bn_aggr(mv[:, t], stats[:, t])
                mean.then_inc(var_ready, 1)
                dve.wait_ge(rstd_ready, b + 1)
                wait(dve, xT_psum, b - 1)
                for t in range(NT):
                    last = dve.tensor_scalar(xn_sb[:, u, t], x_sb[:, u, t], mv[:, t, 0:1], rstd[:, t:t + 1],
                                             ALU.subtract, ALU.mult)
                last.then_inc(xn_ready, 1)
                dve.drain()

            def split(g, par):
                dve.wait_ge(full_ready, g + 1)
                left, part = rest[:, par], parts[:, par]
                dve.tensor_tensor(left, full[:, par], part[:, 0], ALU.subtract)
                dve.drain()
                dve.tensor_copy(part[:, 1], left)
                dve.drain()
                dve.tensor_tensor(part[:, 2], left, part[:, 1], ALU.subtract).then_inc(parts_ready, 1)
                dve.drain()

            def values(g, par, b_sb):
                dve.wait_ge(v_psum, g + 1)
                wait(dve, v_out[par], 8 * (g - par))
                dve.tensor_tensor(va[:, par, :, 0:D], ps[:, 6 + par, 0:C].rearrange("p (h d) -> p h d", d=D),
                                  b_sb[:].rearrange("p (h d) -> p h d", d=D), ALU.add).then_inc(v_ready, 1)

            normalise(0, 0)
            dve.wait_ge(w_ready, 16 * LOADS)
            dve.tensor_copy(scaled[:], bias[:])
            dve.drain()
            dve.tensor_scalar(scaled[:, 0], bias[:, 0], SCALE, None, ALU.mult)
            dve.tensor_scalar(scaled[:, 2], bias[:, 2], SCALE, None, ALU.mult).then_inc(bias_ready, 1)
            dve.wait_ge(consts, 1)
            for g in range(KC):
                split(g, g)
            for t in range(NT):
                values(t, t % 2, bcv_sb)

            def batch(b, u, last):
                for n in range(NCH):
                    split(chunk(b, n), n % 2)
                    if n == 1 and not last:
                        normalise(b + 1, 1 - u)
                for t in range(NT):
                    values(tile(b, t), t % 2, bv_sb)

            batches(dve, batch)


def attend(nc, ps, ident, identb, q_d, k_d, ck_d, v_d, cv_d, y_d):
    TOTAL = B * U
    QK_LOADS = 6
    with ExitStack() as st:
        def sb(name, shape, dt):
            return st.enter_context(nc.sbuf_tensor(name, shape, dt))

        def sem(name):
            return st.enter_context(nc.semaphore("a_" + name))

        qs = sb("qs", [P, U, 2, G, S], BF16)
        ks = sb("ks", [P, U, 1, G, S], BF16)
        ck_all = sb("ck_all", [P, H, B * SC], BF16)
        cks = sb("cks", [P, U, G, SC], BF16)
        vs = sb("vs", [P, U, NT, G * HD], F32)
        cvs = sb("cvs", [P, U, 2, 2 * HD], F32)
        maskb = sb("maskb", [P, P], BF16)
        negm = sb("negm", [P, 2 * G * NT], F32)
        mrest = sb("mrest", [P, 2 * G * NT], F32)
        mparts = sb("mparts", [P, PARTS, 2 * G * NT], BF16)
        mT = sb("mT", [PARTS * 2 * G * NT, P], BF16)
        pt = sb("pt", [P, 2, G, PW], F32)
        ptc = sb("ptc", [P, 2, 2, S], F32)
        o_sb = sb("o_sb", [P, 2, S], F32)
        recip = sb("recip", [P, 2, NT * G], F32)
        y2 = sb("y2", [P, 2, NT * G, D], F32)
        y_sb = sb("y_sb", [P, 2, NT, G * D], F32)

        consts, passed = sem("consts"), sem("passed")
        qk_in = [sem(f"qk_in{r}") for r in range(U)]
        v_in = [sem(f"v_in{r}") for r in range(U)]
        m_in = [sem("m_in0"), sem("m_in1")]
        y_out = [sem("y_out0"), sem("y_out1")]
        a_psum, a_max, m_split, mT_psum, mT_ready = (sem(n) for n in ("a_psum", "a_max", "m_split", "mT_psum", "mT_ready"))
        ck_in, ck_ready = sem("ck_in"), sem("ck_ready")
        b_psum, b_exp, masked = (sem(n) for n in ("b_psum", "b_exp", "masked"))
        o_psum, o_copied, oT_psum, y_ready = (sem(n) for n in ("o_psum", "o_copied", "oT_psum", "y_ready"))
        blk = st.enter_context(nc.Block())

        @blk.sync
        def _(sp):
            def load_qk(a):
                wait(sp, b_psum, NB * (a.s - U))
                heads = slice(a.u * G * S, (a.u + 1) * G * S)
                row = 0
                for n in (3, 2, 1):
                    rows = slice(row, row + n * D)
                    sp.dma_start(qs[rows, a.u].rearrange("p s h n -> p s (h n)"),
                                 q_d[bass.ds(a.b, 1), 0:n * D, :, heads].rearrange("b r s n -> (b r) s n")).then_inc(qk_in[a.u], 16)
                    part = 3 - n
                    sp.dma_start(ks[rows, a.u, 0].rearrange("p h n -> p (h n)"),
                                 k_d[bass.ds(a.b, 1), part * D:(part + 1) * D, 0, heads].to_broadcast([n, D, G * S])
                                 ).then_inc(qk_in[a.u], 16)
                    row += n * D

            def load_v(a):
                wait(sp, o_psum, a.s - U)
                sp.dma_start(vs[:, a.u], v_d[bass.ds(a.b, 1), :, a.u * G * HD:(a.u + 1) * G * HD].rearrange("b (t p) f -> p (b t) f", p=P)).then_inc(v_in[a.u], 16)
                for half in range(2):
                    src = cv_d[bass.ds(a.b * SC, SC), a.u * G * HD:(a.u + 1) * G * HD].rearrange("k (r f) -> k r f", f=2 * HD)
                    sp.dma_start(cvs[half * SC:(half + 1) * SC, a.u, :, half * HD:(half + 1) * HD],
                                 src[:, :, half * HD:(half + 1) * HD]).then_inc(v_in[a.u], 16)

            def load_m(a):
                sp.wait_ge(mT_ready, a.s)
                sp.dma_start(qs[KQ:KM, a.u].rearrange("p s h n -> p (s h n)"), mT[:]).then_inc(m_in[a.u % 2], 16)

            def store_y(a):
                sp.wait_ge(y_ready, a.s)
                sp.dma_start(y_d[bass.ds(a.b, 1), a.u].rearrange("b (t p) f -> p (b t) f", p=P), y_sb[:, a.u % 2]
                             ).then_inc(y_out[a.u % 2], 16)

            def step(a):
                if a.back(-1).exists:
                    load_qk(a.back(-1))
                if a.back(1).exists:
                    load_m(a.back(1))
                if a.exists:
                    load_v(a)
                if a.back(3).exists:
                    store_y(a.back(3))

            sp.wait_ge(consts, 2)
            for i, part in enumerate(KPARTS):
                sp.dma_start(ck_all[i * D:(i + 1) * D].rearrange("p h n -> p (h n)"),
                             ck_d[part * D:(part + 1) * D].rearrange("d h n -> d (h n)")).then_inc(ck_in, 16)
            load_qk(At(0, 0, TOTAL))
            steps(sp, TOTAL, 3, step)
            for par in range(2):
                sp.wait_ge(y_out[par], 8 * TOTAL)

        @blk.gpsimd
        def _(pool):
            pool.memset(cvs[:], 0.0)
            pool.memset(qs[:], 1.0)
            pool.memset(ks[:], 1.0)
            pool.memset(maskb[:], 0.0)
            pool.drain()
            pool.affine_select(out=maskb[:], in_=maskb[:], compare_op=ALU.is_ge, fill=LOW, base=0,
                               pattern=[[-1, P]], channel_multiplier=1).then_inc(consts, 1)

            def copy_ck(a):
                wait(pool, b_psum, NB * (a.s - U))
                pool.tensor_copy(cks[0:KM, a.u], ck_all[0:KM, a.u * G:(a.u + 1) * G, bass.ds(a.b * SC, SC)]).then_inc(ck_ready, 1)

            pool.wait_ge(ck_in, 16 * len(KPARTS))
            pool.wait_ge(consts, 2)
            copy_ck(At(0, 0, TOTAL))

            def step(a):
                if a.back(-1).exists:
                    copy_ck(a.back(-1))
                x = a.back(2)
                if x.exists:
                    wait_apart(pool, b_exp, NB * (x.s - 1) + NB - 1, passed)
                    for j in range(NT):
                        block = pt[:, x.u % 2, :, OFF[j]:OFF[j] + P]
                        pool.affine_select(out=block, in_=block, compare_op=ALU.is_ge, fill=0.0, base=0,
                                           pattern=[[0, G], [1, P]], channel_multiplier=-1).then_inc(masked, 1)

            steps(pool, TOTAL, 3, step)

        @blk.tensor
        def _(pe):
            def scores_by_query(a, k):
                g = NA * (a.s - 1) + k
                bank = (NA * a.u + k) % 2
                wait(pe, a_max, g - 1)
                if k < 11:
                    t = 0 if k < 1 else 1 if k < 3 else 2 if k < 7 else 3
                    first, count = ((0, 4), (0, 2), (2, 2), *((h, 1) for h in range(4)), *((h, 1) for h in range(4)))[k]
                    w = P * (t + 1)
                    for i in range(count):
                        h = first + i
                        pe.matmul(ps[:, bank, i * w:(i + 1) * w], qs[0:KQ, a.u, 0, h, t * P:(t + 1) * P], ks[0:KQ, a.u, 0, h, 0:w],
                                  start=True, stop=False)
                        mm = pe.matmul(ps[:, bank, i * w + t * P:(i + 1) * w], identb[:], maskb[:], start=False, stop=True)
                else:
                    if k == 11:
                        pe.wait_ge(ck_ready, a.s)
                    for i in range(2):
                        t = 2 * (k - 11) + i
                        for h in range(G):
                            at = (i * G + h) * SC
                            mm = pe.matmul(ps[:, bank, at:at + SC], qs[0:KQ, a.u, 1, h, t * P:(t + 1) * P], cks[0:KQ, a.u, h, :],
                                           start=True, stop=True)
                mm.then_inc(a_psum, 1)

            def maxima_to_rows(a):
                pe.wait_ge(m_split, a.s)
                wait(pe, y_ready, a.s - 3)
                pe.transpose(ps[0:mT.shape[0], 7, 0:P // 2].bitcast(BF16), mparts[:].rearrange("p i m -> p (i m)"), identb[:]
                             ).then_inc(mT_psum, 1)

            def scores_by_key(a, k):
                g = NB * (a.s - 1) + k
                bank = 2 + 2 * ((NB * a.u + k) % 2)
                wait(pe, b_exp, g - 1)
                if k == 0:
                    pe.wait_ge(m_in[a.u % 2], a.uses(2, 16) + 16)
                if k == 6:
                    for h in range(G):
                        r = (h % 2) * SC
                        mm = pe.matmul(ps[r:r + SC, bank + h // 2, :], cks[0:KM, a.u, h, :], qs[0:KM, a.u, 1, h, :],
                                       start=True, stop=True)
                else:
                    todo = [(2 * (k // 3) + k % 3, j, j, 0) for j in (0, 1)] if k % 3 < 2 else \
                        [(2 * (k // 3) + i, j, i, OFF[j] - OFF[2]) for i in (0, 1) for j in (2, 3)]
                    for h, j, bk_, at in todo:
                        mm = pe.matmul(ps[:, bank + bk_, at:at + WID[j]], ks[0:KM, a.u, 0, h, j * P:(j + 1) * P],
                                       qs[0:KM, a.u, 0, h, j * P:S], start=True, stop=True)
                mm.then_inc(b_psum, 1)

            def outputs(a, j):
                if j == 0:
                    wait(pe, y_ready, a.s - 1)
                    pe.wait_ge(masked, NT * a.s)
                    pe.wait_ge(v_in[a.u], a.uses(4, 48) + 48)
                for h in range(G):
                    pe.matmul(ps[h * HD:(h + 1) * HD, 6, j * P:S], vs[:, a.u, j, h * HD:(h + 1) * HD],
                              pt[:, a.u % 2, h, OFF[j]:OFF[j] + WID[j]], start=(j == 0), stop=(j == NT - 1))

            def cross_outputs(a):
                pe.wait_ge(b_exp, NB * a.s)
                if a.back(-2).exists:
                    pe.wait_ge(mT_ready, a.s + 2)
                for r in range(2):
                    mm = pe.matmul(ps[r * SC:(r + 1) * SC, 7, :], cvs[:, a.u, r, :], ptc[:, a.u % 2, r, :], start=True, stop=True)
                mm.then_inc(o_psum, 1)

            def outputs_by_token(a):
                pe.wait_ge(o_copied, a.s)
                for i in range(2):
                    for t in range(NT):
                        mm = pe.transpose(ps[:, 6 + i, t * P:(t + 1) * P], o_sb[:, i, t * P:(t + 1) * P], ident[:])
                mm.then_inc(oT_psum, 1)

            def step(a):
                m, b, o = a.back(1), a.back(2), a.back(3)

                def A(*ks_):
                    for k in ks_:
                        if a.exists:
                            if k == 0:
                                pe.wait_ge(qk_in[a.u], a.uses(4, 16 * QK_LOADS) + 16 * QK_LOADS)
                            scores_by_query(a, k)

                def BK(k):
                    if b.exists:
                        scores_by_key(b, k)

                def CO(j):
                    if o.exists:
                        outputs(o, j)

                A(0, 1)
                CO(0)
                BK(0)
                if m.exists:
                    maxima_to_rows(m)
                A(2, 3)
                BK(1)
                CO(1)
                A(4, 5)
                BK(2)
                CO(2)
                A(6, 7)
                BK(3)
                CO(3)
                if o.exists:
                    cross_outputs(o)
                A(8)
                BK(4)
                A(9, 10)
                if o.exists:
                    outputs_by_token(o)
                BK(5)
                A(11, 12)
                BK(6)

            pe.wait_ge(consts, 2)
            steps(pe, TOTAL, 3, step)

        @blk.scalar
        def _(act):
            def exponentials(a, k):
                bank = 2 + 2 * ((NB * a.u + k) % 2)
                act.wait_ge(b_psum, NB * (a.s - 1) + k + 1)
                if k == 0:
                    wait(act, o_psum, a.s - 2)
                two = ps[:, bank:bank + 2, :]
                if k == 6:
                    src, dst = two, ptc[:, a.u % 2]
                elif k % 3 < 2:
                    w = WID[0] + WID[1]
                    src, dst = two.rearrange("p b n -> p (b n)")[:, 0:w], pt[:, a.u % 2, 2 * (k // 3) + k % 3, 0:w]
                else:
                    src, dst = two[:, :, 0:PW - OFF[2]], pt[:, a.u % 2, 2 * (k // 3):2 * (k // 3) + 2, OFF[2]:PW]
                act.activation(dst, src, ACT.Exp).then_inc(b_exp, 1)

            def step(a):
                b, o = a.back(2), a.back(3)
                for k in range(NB):
                    if b.exists:
                        exponentials(b, k)
                    if k == 3 and o.exists:
                        act.wait_ge(o_psum, o.s)
                        wait(act, oT_psum, o.s - 1)
                        act.copy(o_sb[:, 0], ps[:, 6, :])
                        act.copy(o_sb[:, 1], ps[:, 7, :]).then_inc(o_copied, 1)

            steps(act, TOTAL, 3, step)

        @blk.vector
        def _(dve):
            def maxima(a, k):
                bank = (NA * a.u + k) % 2
                dve.wait_ge(a_psum, NA * (a.s - 1) + k + 1)
                if k == 0:
                    dst, src = negm[:, 0:G * NT:NT], ps[:, bank, :].rearrange("p (h n) -> p h n", h=G)
                elif k < 3:
                    lo = 2 * (k - 1) * NT + 1
                    dst, src = negm[:, lo:lo + NT + 1:NT], ps[:, bank, :].rearrange("p (h n) -> p h n", h=2)
                elif k < 11:
                    h, t = (k - 3) % 4, 2 + (k - 3) // 4
                    dst, src = negm[:, h * NT + t:h * NT + t + 1], ps[:, bank, 0:(t + 1) * P]
                else:
                    t = 2 * (k - 11)
                    dst = negm[:, G * NT:].rearrange("p (h t) -> p t h", t=NT)[:, t:t + 2, :]
                    src = ps[:, bank, :].rearrange("p (t h n) -> p t h n", t=2, h=G)
                dve.tensor_reduce(dst, src, AX.X, ALU.max, negate=True).then_inc(a_max, 1)

            def split_maxima(a):
                dve.drain()
                dve.tensor_copy(mparts[:, 0], negm[:])
                dve.drain()
                dve.tensor_tensor(mrest[:], negm[:], mparts[:, 0], ALU.subtract)
                dve.drain()
                dve.tensor_copy(mparts[:, 1], mrest[:])
                dve.drain()
                dve.tensor_tensor(mparts[:, 2], mrest[:], mparts[:, 1], ALU.subtract).then_inc(m_split, 1)
                dve.drain()

            def copy_maxima(a):
                dve.wait_ge(mT_psum, a.s)
                if a.back(1).exists:
                    x = a.back(1)
                    wait(dve, m_in[x.u % 2], x.uses(2, 16) + 16)
                dve.tensor_copy(mT[:], ps[0:mT.shape[0], 7, 0:P // 2].bitcast(BF16)).then_inc(mT_ready, 1)

            def normalise(a):
                dve.wait_ge(oT_psum, a.s)
                wait(dve, y_out[a.u % 2], a.uses(2, 16))
                for i in range(2):
                    heads = ps[:, 6 + i, :].rearrange("p (x f) -> p x f", f=HD)
                    dve.reciprocal(recip[:, i].rearrange("p (x o) -> p x o", o=1), heads[:, :, D:D + 1])
                dve.drain()
                for i in range(2):
                    heads = ps[:, 6 + i, :].rearrange("p (x f) -> p x f", f=HD)
                    dve.tensor_tensor(y2[:, i], heads[:, :, 0:D],
                                      recip[:, i].rearrange("p (x o) -> p x o", o=1).to_broadcast([P, NT * G, D]), ALU.mult)
                dve.drain()
                dve.tensor_tensor(y_sb[:, a.u % 2].rearrange("p t f -> p (t f)"), y2[:, 0].rearrange("p x d -> p (x d)"),
                                  y2[:, 1].rearrange("p x d -> p (x d)"), ALU.add).then_inc(y_ready, 1)
                dve.drain()

            def step(a):
                m, o = a.back(1), a.back(3)
                for k in range(NA):
                    if a.exists:
                        maxima(a, k)
                    if k == 1 and m.exists:
                        copy_maxima(m)
                    if k == 10 and o.exists:
                        normalise(o)
                if a.exists:
                    split_maxima(a)

            dve.memset(ck_all[:], 1.0).then_inc(consts, 1)
            steps(dve, TOTAL, 3, step)


def route(nc, ps, ident, x, Wp, bp, gate_w, gate_b, w1, w2, b2, y_d, xn_d, tab_d, b2_d, out,
          w1_sb, w2_sb, w_in):
    TOTAL = N // P
    with ExitStack() as st:
        def sb(name, shape, dt):
            return st.enter_context(nc.sbuf_tensor(name, shape, dt))

        def sem(name):
            return st.enter_context(nc.semaphore("r_" + name))

        wp_sb = sb("wp_sb", [P, KC, C], F32)
        gw_sb = sb("gw_sb", [P, KC, E], F32)
        bp_sb = sb("bp_sb", [P, C], F32)
        gb_sb = sb("gb_sb", [P, E], F32)
        b2_sb, b2_rest = sb("b2_sb", [E, C], F32), sb("b2_rest", [E, C], F32)
        b2_parts = sb("b2_parts_sb", [E, PARTS, C], BF16)
        before = sb("before", [P, P], BF16)
        ones = sb("ones", [P, P], BF16)
        expert = sb("expert", [P, E], F32)
        token = sb("token", [P, 1], F32)
        y_in = sb("y_in_sb", [P, U, U, G * D], F32)
        x_in_sb = sb("x_in_sb", [P, U, C], F32)
        xb = sb("xb", [P, U, C], F32)
        yT = sb("yT", [P, U, KC, P], F32)
        x1 = sb("x1", [P, U, C], F32)
        stats, mv = sb("r_stats", [P, 6], F32), sb("r_mv", [P, U, 2], F32)
        base, rstd, power = sb("r_base", [P, 1], F32), sb("r_rstd", [P, U], F32), sb("r_power", [P, 1], F32)
        xn = sb("xn", [P, U, C], F32)
        xnT = sb("xnT", [P, U, KC, P], F32)
        lg = sb("lg", [P, U, E], F32)
        top = sb("top", [P, U, 8], F32)
        top_i = sb("top_i", [P, U, 8], U32)
        top_f = sb("top_f", [P, U, TOPK], F32)
        neg_top = sb("neg_top", [P, U], F32)
        hot = sb("hot", [P, U, TOPK, E], F32)
        chosen = sb("chosen", [P, U, E], BF16)
        sofar = sb("sofar", [P, U, E], BF16)
        picked = sb("picked", [P, TOPK, E], F32)
        place = sb("place", [P, TOPK], F32)
        slot = sb("slot", [P, U, TOPK], U32)
        eg = sb("eg", [P, U, TOPK], F32)
        esum = sb("esum", [P, U], F32)
        einv = sb("einv", [P, 1], F32)
        row = sb("row", [P, U, TOPK, 2], I32)

        consts, w_ready, passed = sem("consts"), sem("w_ready"), sem("passed")
        b2_ready, b2_out = sem("b2_ready"), sem("b2_out")
        loaded = [sem(f"loaded{r}") for r in range(U)]
        x1_out = [sem(f"x1_out{r}") for r in range(U)]
        table_out = [sem(f"table_out{r}") for r in range(U)]
        xb_ready, yT_psum, yT_ready, p_psum, x1_ready = (sem(n) for n in ("xb", "yT_psum", "yT_ready", "p_psum", "x1"))
        var_ready, rstd_ready, xn_ready, xnT_psum, xnT_ready = (sem(n) for n in ("var", "rstd", "xn", "xnT_psum", "xnT_ready"))
        lg_psum, top_ready, hot_ready, exp_ready, place_psum, row_ready = (
            sem(n) for n in ("lg_psum", "top", "hot", "exp", "place_psum", "row"))
        LOADS = 4
        blk = st.enter_context(nc.Block())

        @blk.sync
        def _(sp):
            sp.dma_start(wp_sb[:], Wp.rearrange("(c p) n -> p c n", p=P)).then_inc(w_ready, 16)
            sp.dma_start(bp_sb[:], bp.rearrange("(a c) -> a c", a=1).to_broadcast([P, C])).then_inc(w_ready, 16)
            sp.dma_start(gw_sb[:], gate_w.rearrange("(c p) n -> p c n", p=P)).then_inc(w_ready, 16)
            sp.dma_start(gb_sb[:], gate_b.rearrange("(a c) -> a c", a=1).to_broadcast([P, E])).then_inc(w_ready, 16)

            def load(a):
                wait(sp, yT_psum, a.s - U)
                wait(sp, xb_ready, a.s - U)
                sp.dma_start(y_in[:, a.u], y_d[bass.ds(a.b, 1), :, a.u * P:(a.u + 1) * P, :].rearrange("b g t f -> t (b g) f")
                             ).then_inc(loaded[a.u], 16)
                sp.dma_start(x_in_sb[:, a.u], x[bass.ds(a.b, 1), a.u * P:(a.u + 1) * P, :].rearrange("b t c -> (b t) c")
                             ).then_inc(loaded[a.u], 16)

            def store(a):
                sp.wait_ge(xn_ready, a.s)
                sp.dma_start(out[bass.ds(a.b * S + a.u * P, P), :], x1[:, a.u]).then_inc(x1_out[a.u], 16)
                sp.dma_start(xn_d[bass.ds(a.b * S + a.u * P, P), :], xn[:, a.u]).then_inc(x1_out[a.u], 16)

            def step(a):
                if a.back(-1).exists:
                    load(a.back(-1))
                if a.back(1).exists:
                    store(a.back(1))

            load(At(0, 0, TOTAL))
            sp.dma_start(b2_sb[:], b2).then_inc(b2_out, 16)
            steps(sp, TOTAL, 4, step)
            for e in range(U):
                load_expert(sp, w1, w2, w1_sb, w2_sb, w_in, e, e)
            sp.wait_ge(b2_ready, 1)
            sp.dma_start(b2_d.rearrange("i e c -> e i c"), b2_parts[:]).then_inc(b2_out, 16)
            sp.wait_ge(b2_out, 32)
            for r in range(U):
                sp.wait_ge(x1_out[r], 32 * (TOTAL // U))

        @blk.gpsimd
        def _(pool):
            pool.memset(before[:], 1.0)
            pool.memset(ones[:], 1.0)
            pool.memset(sofar[:], 0.0)
            pool.memset(power[:], -0.5)
            pool.iota(expert[:], pattern=[[1, E]], base=0, channel_multiplier=0, allow_small_or_imprecise_dtypes=True)
            pool.iota(token[:], pattern=[[0, 1]], base=0, channel_multiplier=1, allow_small_or_imprecise_dtypes=True)
            pool.drain()
            pool.affine_select(out=before[:], in_=before[:], compare_op=ALU.is_gt, fill=0.0, base=0,
                               pattern=[[1, P]], channel_multiplier=-1).then_inc(consts, 1)
            pool.wait_ge(w_ready, 16 * LOADS)

            def add_bias(a):
                pool.wait_ge(loaded[a.u], a.uses(4, 32) + 32)
                wait(pool, x1_ready, a.s - U)
                pool.tensor_tensor(xb[:, a.u], x_in_sb[:, a.u], bp_sb[:], ALU.add).then_inc(xb_ready, 1)

            def deviation(a):
                pool.wait_ge(var_ready, a.s)
                wait_apart(pool, xn_ready, a.s - U, passed)
                pool.tensor_scalar(base[:], mv[:, a.u, 1:2], EPS, None, ALU.add)
                pool.drain()
                pool.tensor_tensor(rstd[:, a.u:a.u + 1], base[:], power[:], ALU.pow).then_inc(rstd_ready, 1)
                pool.drain()

            def scatter(a):
                wait_apart(pool, row_ready, a.s, passed)
                for k in range(TOPK):
                    pool.indirect_dma_start(out=tab_d, out_offset=bass.IndirectOffsetOnAxis(ap=slot[:, a.u, k:k + 1], axis=0),
                                            in_=row[:, a.u, k, :], in_offset=None, bounds_check=CAP * E - 1,
                                            oob_is_err=False).then_inc(table_out[a.u], 16)

            def step(a):
                if a.exists:
                    add_bias(a)
                if a.back(1).exists:
                    deviation(a.back(1))
                if a.back(4).exists:
                    scatter(a.back(4))

            steps(pool, TOTAL, 4, step)
            for r in range(U):
                pool.wait_ge(table_out[r], 16 * TOPK * (TOTAL // U))

        @blk.tensor
        def _(pe):
            pe.wait_ge(w_ready, 16 * LOADS)
            pe.wait_ge(consts, 1)

            def step(a):
                if a.exists:
                    pe.wait_ge(loaded[a.u], a.uses(4, 32) + 32)
                    wait(pe, yT_ready, a.s - 1)
                    for c in range(KC):
                        mm = pe.transpose(ps[:, 0, c * P:(c + 1) * P],
                                          y_in[:, a.u].rearrange("p g f -> p (g f)")[:, c * P:(c + 1) * P], ident[:])
                    mm.then_inc(yT_psum, 1)
                x_ = a.back(1)
                if x_.exists:
                    pe.wait_ge(yT_ready, x_.s)
                    wait(pe, x1_ready, x_.s - 1)
                    for c in range(KC):
                        mm = pe.matmul(ps[:, 1, 0:C], yT[:, x_.u, c, :], wp_sb[:, c, :], start=(c == 0), stop=(c == KC - 1))
                    mm.then_inc(p_psum, 1)
                x_ = a.back(2)
                if x_.exists:
                    pe.wait_ge(xn_ready, x_.s)
                    wait(pe, xnT_ready, x_.s - 1)
                    for c in range(KC):
                        mm = pe.transpose(ps[:, 2, c * P:(c + 1) * P], xn[:, x_.u, c * P:(c + 1) * P], ident[:])
                    mm.then_inc(xnT_psum, 1)
                x_ = a.back(3)
                if x_.exists:
                    pe.wait_ge(xnT_ready, x_.s)
                    wait(pe, top_ready, x_.s - 1)
                    for c in range(KC):
                        mm = pe.matmul(ps[:, 3, 0:E], xnT[:, x_.u, c, :], gw_sb[:, c, :], start=(c == 0), stop=(c == KC - 1))
                    mm.then_inc(lg_psum, 1)
                x_ = a.back(4)
                if x_.exists:
                    pe.wait_ge(hot_ready, x_.s)
                    wait(pe, row_ready, x_.s - 1)
                    pe.matmul(ps[:, 4, 0:E], before[:], chosen[:, x_.u, :], start=True, stop=False)
                    pe.matmul(ps[:, 4, 0:E], ones[:], sofar[:, x_.u, :], start=False, stop=True).then_inc(place_psum, 1)

            steps(pe, TOTAL, 4, step)

        @blk.scalar
        def _(act):
            def step(a):
                if a.exists:
                    act.wait_ge(yT_psum, a.s)
                    wait(act, p_psum, a.s - U)
                    act.copy(yT[:, a.u].rearrange("p c n -> p (c n)"), ps[:, 0, 0:C]).then_inc(yT_ready, 1)
                x_ = a.back(2)
                if x_.exists:
                    act.wait_ge(xnT_psum, x_.s)
                    wait(act, lg_psum, a.s - 5)
                    act.copy(xnT[:, x_.u].rearrange("p c n -> p (c n)"), ps[:, 2, 0:C]).then_inc(xnT_ready, 1)
                x_ = a.back(3)
                if x_.exists:
                    act.wait_ge(hot_ready, x_.s)
                    wait(act, row_ready, a.s - 5)
                    act.activation(eg[:, x_.u], top[:, x_.u, 0:TOPK], ACT.Exp, bias=neg_top[:, x_.u:x_.u + 1],
                                   accum_out=esum[:, x_.u:x_.u + 1]).then_inc(exp_ready, 1)

            steps(act, TOTAL, 4, step)

        @blk.vector
        def _(dve):
            dve.wait_ge(b2_out, 16)
            dve.tensor_copy(b2_parts[:, 0], b2_sb[:])
            dve.drain()
            dve.tensor_tensor(b2_rest[:], b2_sb[:], b2_parts[:, 0], ALU.subtract)
            dve.drain()
            dve.tensor_copy(b2_parts[:, 1], b2_rest[:])
            dve.drain()
            dve.tensor_tensor(b2_parts[:, 2], b2_rest[:], b2_parts[:, 1], ALU.subtract).then_inc(b2_ready, 1)
            dve.wait_ge(w_ready, 16 * LOADS)
            dve.wait_ge(consts, 1)

            def residual(a):
                dve.wait_ge(p_psum, a.s)
                dve.wait_ge(xb_ready, a.s)
                wait(dve, x1_out[a.u], a.uses(4, 32))
                dve.tensor_tensor(x1[:, a.u], ps[:, 1, 0:C], xb[:, a.u], ALU.add).then_inc(x1_ready, 1)
                dve.drain()
                dve.bn_stats(stats[:], x1[:, a.u])
                dve.drain()
                dve.bn_aggr(mv[:, a.u], stats[:]).then_inc(var_ready, 1)
                dve.drain()

            def normalise(a):
                dve.wait_ge(rstd_ready, a.s)
                dve.tensor_scalar(xn[:, a.u], x1[:, a.u], mv[:, a.u, 0:1], rstd[:, a.u:a.u + 1],
                                  ALU.subtract, ALU.mult).then_inc(xn_ready, 1)

            def choose(a):
                dve.wait_ge(lg_psum, a.s)
                wait(dve, place_psum, a.s - 2)
                dve.tensor_tensor(lg[:, a.u], ps[:, 3, 0:E], gb_sb[:], ALU.add).then_inc(top_ready, 1)
                dve.drain()
                dve.max(top[:, a.u], lg[:, a.u])
                dve.drain()
                dve.max_index(top_i[:, a.u], top[:, a.u], lg[:, a.u])
                dve.tensor_scalar(neg_top[:, a.u:a.u + 1], top[:, a.u, 0:1], -1.0, None, ALU.mult)
                dve.drain()
                dve.tensor_copy(top_f[:, a.u], top_i[:, a.u, 0:TOPK])
                dve.drain()
                dve.tensor_tensor(hot[:, a.u], expert[:].rearrange("p (o e) -> p o e", o=1).to_broadcast([P, TOPK, E]),
                                  top_f[:, a.u].rearrange("p (k o) -> p k o", o=1).to_broadcast([P, TOPK, E]), ALU.is_equal)
                dve.drain()
                with nc.allow_low_precision(reason="counts up to three are exact"):
                    dve.tensor_reduce(chosen[:, a.u], hot[:, a.u].rearrange("p k e -> p e k"), AX.X, ALU.add)
                dve.drain()
                dve.tensor_tensor(sofar[:, (a.u + 1) % U], sofar[:, a.u], chosen[:, a.u], ALU.add).then_inc(hot_ready, 1)
                dve.drain()

            def enter(a):
                dve.wait_ge(place_psum, a.s)
                dve.wait_ge(exp_ready, a.s)
                wait(dve, table_out[a.u], a.uses(4, 16 * TOPK))
                dve.tensor_tensor(picked[:], hot[:, a.u], ps[:, 4, 0:E].rearrange("p (o e) -> p o e", o=1).to_broadcast([P, TOPK, E]),
                                  ALU.mult)
                dve.reciprocal(einv[:], esum[:, a.u:a.u + 1])
                dve.drain()
                dve.tensor_reduce(place[:], picked[:], AX.X, ALU.add)
                dve.tensor_scalar(row[:, a.u, :, 1].bitcast(F32), eg[:, a.u], einv[:, 0:1], None, ALU.mult)
                dve.tensor_copy(row[:, a.u, :, 0], token[:].to_broadcast([P, TOPK]))
                dve.drain()
                dve.tensor_scalar(token[:], token[:], float(P), None, ALU.add)
                dve.scalar_tensor_tensor(out=slot[:, a.u], in0=place[:], scalar=float(E), in1=top_f[:, a.u],
                                         op0=ALU.mult, op1=ALU.add).then_inc(row_ready, 1)
                dve.drain()

            def step(a):
                if a.back(1).exists:
                    residual(a.back(1))
                if a.back(4).exists:
                    enter(a.back(4))
                if a.back(1).exists:
                    normalise(a.back(1))
                if a.back(3).exists:
                    choose(a.back(3))

            steps(dve, TOTAL, 4, step)


def experts(nc, ps, ident, w1, b1, w2, xn_d, tab_d, b2_d, out, w1_sb, w2_sb, w_in):
    with ExitStack() as st:
        def sb(name, shape, dt):
            return st.enter_context(nc.sbuf_tensor(name, shape, dt))

        def sem(name):
            return st.enter_context(nc.semaphore("e_" + name))

        tab = sb("tab", [P, E, 2], I32)
        b1_rows = sb("b1_rows", [P, E * FC // P, P], F32)
        b1T = sb("b1T", [P, E * FC], F32)
        b2p = sb("b2p", [PARTS, E * C], BF16)
        ones3 = sb("ones3", [PARTS, P], BF16)
        from_ids, to_ids = sb("from_ids", [P, U], I32), sb("to_ids", [P, U], I32)
        xg = sb("xg", [P, U, C], F32)
        xgT = sb("xgT", [P, 2, KC, P], F32)
        hT = sb("hT", [P, 2, FC, P], F32)
        yg = sb("yg", [P, U, C], F32)

        setup, tab_in, ones_ready = sem("setup"), sem("tab_in"), sem("ones")
        b1_psum, b1_ready = sem("b1_psum"), sem("b1_ready")
        ids_ready, to_ready = sem("ids"), sem("to_ready")
        gathered = [sem(f"gathered{r}") for r in range(U)]
        added, passed = sem("added"), sem("passed")
        xT_psum, xT_ready, h_psum, h_ready, y_psum, y_ready = (
            sem(n) for n in ("xT_psum", "xT_ready", "h_psum", "h_ready", "y_psum", "y_ready"))
        blk = st.enter_context(nc.Block())

        @blk.sync
        def _(sp):
            sp.dma_start(tab[:].rearrange("p e t -> p (e t)"), tab_d.rearrange("(p e) t -> p (e t)", p=P)).then_inc(tab_in, 16)
            sp.dma_start(b1_rows[:], b1.rearrange("e (c p) -> (e c) p", p=P).rearrange("(g q) p -> q g p", q=P)).then_inc(setup, 16)
            sp.dma_start(b2p[:], b2_d.rearrange("i e c -> i (e c)")).then_inc(setup, 16)

            def step(a):
                if a.exists and not (isinstance(a.s, int) and a.s <= U):
                    sp.wait_ge(y_psum, a.s - U)
                    load_expert(sp, w1, w2, w1_sb, w2_sb, w_in, a.b * U + a.u, a.u)

            steps(sp, E, 1, step)

        @blk.gpsimd
        def _(pool):
            pool.memset(ones3[:], 1.0).then_inc(ones_ready, 1)
            pool.wait_ge(tab_in, 16)

            def gather(a):
                wait(pool, xT_psum, a.s - U)
                wait_apart(pool, gathered[a.u], a.uses(4, 16), passed)
                pool.tensor_copy(from_ids[:, a.u:a.u + 1], tab[:, bass.ds(a.b * U + a.u, 1), 0]).then_inc(ids_ready, 1)
                wait_apart(pool, ids_ready, a.s, passed)
                pool.indirect_dma_start(out=xg[:, a.u], out_offset=None, in_=xn_d,
                                        in_offset=bass.IndirectOffsetOnAxis(ap=from_ids[:, a.u:a.u + 1].bitcast(U32), axis=0),
                                        bounds_check=N + P - 1).then_inc(gathered[a.u], 16)

            def add(a):
                wait_apart(pool, added, 16 * (a.s - 1), passed)
                pool.tensor_copy(to_ids[:, a.u:a.u + 1], tab[:, bass.ds(a.b * U + a.u, 1), 0]).then_inc(to_ready, 1)
                pool.wait_ge(to_ready, a.s)
                wait_apart(pool, y_ready, a.s, passed)
                pool.indirect_dma_start(out=out, out_offset=bass.IndirectOffsetOnAxis(ap=to_ids[:, a.u:a.u + 1].bitcast(U32), axis=0),
                                        in_=yg[:, a.u], in_offset=None, bounds_check=N + P - 1, compute_op=ALU.add
                                        ).then_inc(added, 16)

            def step(a):
                if a.back(-3).exists:
                    gather(a.back(-3))
                if a.back(1).exists:
                    add(a.back(1))

            for u in range(3):
                gather(At(0, u, E))
            steps(pool, E, 1, step)
            pool.wait_ge(added, 16 * E)

        @blk.tensor
        def _(pe):
            def tokens_by_channel(a):
                pe.wait_ge(gathered[a.u], a.uses(4, 16) + 16)
                wait(pe, xT_ready, a.s - 2)
                for c in range(KC):
                    mm = pe.transpose(ps[:, a.u % 2, c * P:(c + 1) * P], xg[:, a.u, c * P:(c + 1) * P], ident[:])
                mm.then_inc(xT_psum, 1)

            def first_layer(a):
                pe.wait_ge(w_in[a.u], a.uses(4, 32) + 32)
                pe.wait_ge(xT_ready, a.s)
                for n in range(FC):
                    if n % 4 == 0:
                        wait(pe, h_ready, FC * (a.s - 2))
                    for c in range(KC):
                        mm = pe.matmul(ps[:, 2 + 2 * (a.u % 2) + n // 4, (n % 4) * P:(n % 4 + 1) * P],
                                       w1_sb[:, a.u, c, n * P:(n + 1) * P], xgT[:, a.u % 2, c, :], start=(c == 0), stop=(c == KC - 1))
                    if n % 4 == 3:
                        mm.then_inc(h_psum, 1)

            def second_layer(a):
                pe.wait_ge(h_ready, FC * a.s)
                wait(pe, y_ready, a.s - 2)
                bank = ps[:, 6 + a.u % 2, 0:C]
                pe.matmul(bank, ones3[:], b2p[:, bass.ds((a.b * U + a.u) * C, C)], start=True, stop=False)
                for n in range(FC):
                    mm = pe.matmul(bank, hT[:, a.u % 2, n, :], w2_sb[:, a.u, n, :], start=False, stop=(n == FC - 1))
                mm.then_inc(y_psum, 1)

            pe.wait_ge(setup, 32)
            pe.wait_ge(ones_ready, 1)
            for g in range(E * FC // P):
                mm = pe.transpose(ps[:, 7, g * P:(g + 1) * P], b1_rows[:, g, :], ident[:])
            mm.then_inc(b1_psum, 1)
            tokens_by_channel(At(0, 0, E))
            pe.wait_ge(b1_ready, 1)

            def step(a):
                if a.back(-1).exists:
                    tokens_by_channel(a.back(-1))
                if a.exists:
                    first_layer(a)
                if a.back(1).exists:
                    second_layer(a.back(1))

            steps(pe, E, 1, step)

        @blk.scalar
        def _(act):
            act.wait_ge(b1_psum, 1)
            act.copy(b1T[:], ps[:, 7, :]).then_inc(b1_ready, 1)
            act.wait_ge(b1_ready, 1)

            def step(a):
                if a.exists:
                    for n in range(FC):
                        if n % 4 == 0:
                            act.wait_ge(h_psum, FC // 4 * (a.s - 1) + n // 4 + 1)
                        if n == 0:
                            wait(act, y_psum, a.s - 2)
                        act.activation(hT[:, a.u % 2, n, :], ps[:, 2 + 2 * (a.u % 2) + n // 4, (n % 4) * P:(n % 4 + 1) * P],
                                       ACT.Gelu, bias=b1T[:, bass.ds((a.b * U + a.u) * FC + n, 1)]).then_inc(h_ready, 1)

            steps(act, E, 1, step)

        @blk.vector
        def _(dve):
            dve.wait_ge(tab_in, 16)

            def copy_tokens(a):
                dve.wait_ge(xT_psum, a.s)
                wait(dve, h_psum, FC // 4 * (a.s - 2))
                dve.tensor_copy(xgT[:, a.u % 2].rearrange("p c n -> p (c n)"), ps[:, a.u % 2, 0:C]).then_inc(xT_ready, 1)

            def scale_rows(a):
                dve.wait_ge(y_psum, a.s)
                wait(dve, added, 16 * (a.s - U))
                dve.tensor_scalar(yg[:, a.u], ps[:, 6 + a.u % 2, 0:C],
                                  tab[:, bass.ds(a.b * U + a.u, 1), 1].bitcast(F32), None, ALU.mult).then_inc(y_ready, 1)

            copy_tokens(At(0, 0, E))

            def step(a):
                if a.back(-1).exists:
                    copy_tokens(a.back(-1))
                if a.back(1).exists:
                    scale_rows(a.back(1))

            steps(dve, E, 1, step)


_INS = ["x", "ctx_512", "L0_xattn_Wk", "L0_xattn_bk", "L0_xattn_Wq", "L0_xattn_bq", "L0_xattn_Wv", "L0_xattn_bv",
        "L0_xattn_Wck", "L0_xattn_bck", "L0_xattn_Wcq", "L0_xattn_bcq", "L0_xattn_Wcv", "L0_xattn_bcv",
        "L0_xattn_Wp", "L0_xattn_bp", "L0_ffn_gate_w", "L0_ffn_gate_b", "L0_ffn_w1", "L0_ffn_b1", "L0_ffn_w2", "L0_ffn_b2"]


def kernel(**inputs):
    import numpy as np
    import concourse.bacc as bacc
    from concourse.bass_utils import run_bass_kernel_spmd

    nc = bacc.Bacc("TRN2", target_bir_lowering=False, num_devices=1)
    arrays, args = {}, []
    for name in _INS:
        a = np.ascontiguousarray(inputs[name])
        arrays[f"in_{name}"] = a
        args.append(nc.dram_tensor(f"in_{name}", a.shape, mybir.dt.from_np(a.dtype), kind="ExternalInput").ap())
    out = nc.dram_tensor("out_rows", (N + P, C), F32, kind="ExternalOutput").ap()
    layer_kernel(nc, *args, out)
    r = run_bass_kernel_spmd(nc, [arrays], core_ids=[0])
    return r.results[0]["out_rows"][:N].reshape(B, S, C)
```

```python
from contextlib import ExitStack

import concourse.bass as bass
from concourse import mybir

ALU = mybir.AluOpType
ACT = mybir.ActivationFunctionType
AX = mybir.AxisListType
F32 = mybir.dt.float32
BF16 = mybir.dt.bfloat16
I32 = mybir.dt.int32
U32 = mybir.dt.uint32

P = 128
B, S, C = 8, 512, 256
CC, SC = 128, 64
H, D = 16, 16
G = 4
U = H // G
NT = S // P
KC = C // P
N = B * S
E, TOPK, CAP, F = 64, 3, 128, 1024
FC = F // P
EPS = 1e-5
PARTS = 3
QPARTS = (0, 1, 2, 0, 1, 0)
KPARTS = (0, 0, 0, 1, 1, 2)
KQ = len(KPARTS) * D
KM = KQ + PARTS
HD = 32
WID = [S - P * j for j in range(NT)]
OFF = [sum(WID[:j]) for j in range(NT)]
PW = sum(WID)
NA, NB = 13, 7
SCALE = D ** -0.5
LOW = -1e30


def wait(eng, sem, value):
    if not isinstance(value, int) or value > 0:
        eng.wait_ge(sem, value)


def wait_apart(pool, sem, value, passed):
    wait(pool, sem, value)
    pool.sem_inc(passed, 1)


class At:

    def __init__(self, b, u, total):
        self.b, self.u, self.total = b, u, total
        self.s = b * U + u + 1
        self.exists = not isinstance(self.s, int) or 1 <= self.s <= total

    def back(self, k):
        if isinstance(self.b, int):
            s = self.s - k - 1
            return At(s // U, s % U, self.total)
        carry = (self.u - k) // U
        return At(self.b + carry, (self.u - k) % U, self.total)

    def uses(self, ring, each):
        return (self.s - 1 - self.u % ring) * (each // ring)


def steps(eng, total, extra, body):
    for s in range(2 * U):
        body(At(s // U, s % U, total))
    with eng.Fori(2, total // U - 1, 1) as b:
        for u in range(U):
            body(At(b, u, total))
    for s in range(total - U, total + extra):
        body(At(s // U, s % U, total))


def layer_kernel(nc, x, ctx, Wk, bk, Wq, bq, Wv, bv, Wck, bck, Wcq, bcq, Wcv, bcv, Wp, bp,
                 gate_w, gate_b, w1, b1, w2, b2, out):
    def dram(name, shape, dt):
        return nc.dram_tensor(name, shape, dt).ap()

    q_d = dram("q_parts", [B, PARTS * D, 2, H * S], BF16)
    k_d = dram("k_parts", [B, PARTS * D, 1, H * S], BF16)
    ck_d = dram("ck_parts", [PARTS * D, H, B * SC], BF16)
    v_d = dram("v_rows", [B, S, H * HD], F32)
    cv_d = dram("cv_rows", [B * SC, H * HD], F32)
    y_d = dram("attention", [B, U, S, G * D], F32)
    xn_d = dram("xn_rows", [N + P, C], F32)
    tab_d = dram("slot_table", [CAP * E, 2], I32)
    b2_d = dram("b2_parts", [PARTS, E, C], BF16)

    with ExitStack() as whole:
        ps = whole.enter_context(nc.psum_tensor("ps", [P, 8, 512], F32))
        ident = whole.enter_context(nc.sbuf_tensor("ident", [P, P], F32))
        identb = whole.enter_context(nc.sbuf_tensor("identb", [P, P], BF16))
        w1_sb = whole.enter_context(nc.sbuf_tensor("w1_sb", [P, U, KC, F], F32))
        w2_sb = whole.enter_context(nc.sbuf_tensor("w2_sb", [P, U, FC, C], F32))
        ks = whole.enter_context(nc.sbuf_tensor("ks", [P, U, 1, G, S], BF16))
        cks = whole.enter_context(nc.sbuf_tensor("cks", [P, U, G, SC], BF16))
        cvs = whole.enter_context(nc.sbuf_tensor("cvs", [P, U, 2, 2 * HD], F32))
        maskb = whole.enter_context(nc.sbuf_tensor("maskb", [P, P], BF16))
        w_in = [whole.enter_context(nc.semaphore(f"w_in{r}")) for r in range(U)]

        project(nc, ps, ident, identb, x, ctx, Wk, bk, Wq, bq, Wv, bv, Wck, bck, Wcq, bcq, Wcv, bcv,
                q_d, k_d, ck_d, v_d, cv_d, xn_d, tab_d, out, ks, cks, cvs, maskb)
        attend(nc, ps, ident, identb, ks, cks, cvs, maskb, q_d, k_d, ck_d, v_d, cv_d, y_d, w1, w2, w1_sb, w2_sb, w_in)
        route(nc, ps, ident, x, Wp, bp, gate_w, gate_b, b2, y_d, xn_d, tab_d, b2_d, out)
        experts(nc, ps, ident, w1, b1, w2, xn_d, tab_d, b2_d, out, w1_sb, w2_sb, w_in)


def load_expert(eng, w1, w2, w1_sb, w2_sb, w_in, e, ring):
    eng.dma_start(w1_sb[:, ring], w1[bass.ds(e, 1)].rearrange("e (c p) f -> p (e c) f", p=P)).then_inc(w_in[ring], 16)
    eng.dma_start(w2_sb[:, ring], w2[bass.ds(e, 1)].rearrange("e (c p) d -> p (e c) d", p=P)).then_inc(w_in[ring], 16)


def project(nc, ps, ident, identb, x, ctx, Wk, bk, Wq, bq, Wv, bv, Wck, bck, Wcq, bcq, Wcv, bcv,
            q_d, k_d, ck_d, v_d, cv_d, xn_d, tab_d, out, ks, cks, cvs, maskb):
    NCH = 3 * KC
    RING = NCH
    with ExitStack() as st:
        def sb(name, shape, dt):
            return st.enter_context(nc.sbuf_tensor(name, shape, dt))

        def sem(name):
            return st.enter_context(nc.semaphore("p_" + name))

        wq_sb, wk_sb, wcq_sb, wv_sb = (sb(n, [P, KC, C], F32) for n in ("wq_sb", "wk_sb", "wcq_sb", "wv_sb"))
        wck_sb, wcv_sb = (sb(n, [P, C], F32) for n in ("wck_sb", "wcv_sb"))
        bias = sb("bias", [P, 4, KC], F32)
        scaled = sb("scaled", [P, 4, KC], F32)
        bv_sb, bcv_sb = (sb(n, [P, C], F32) for n in ("bv_sb", "bcv_sb"))
        x_sb = sb("x_sb", [P, 2, NT, C], F32)
        xn_sb = sb("xn_sb", [P, 2, NT, C], F32)
        xT = sb("xT", [P, 2, KC, S], F32)
        cx = sb("cx", [P, NT, CC], F32)
        cxT = sb("cxT", [P, S], F32)
        stats = sb("stats", [P, NT, 6], F32)
        mv = sb("mv", [P, NT, 2], F32)
        base = sb("base", [P, NT], F32)
        rstd = sb("rstd", [P, NT], F32)
        power = sb("power", [P, NT], F32)
        full = sb("full", [P, RING, S], F32)
        rest = sb("rest", [P, RING, S], F32)
        parts = sb("parts", [P, RING, PARTS, S], BF16)
        va = sb("va", [P, NT, H, HD], F32)
        zero = sb("zero", [P, C], F32)
        ids = sb("ids", [P, E, 2], I32)

        consts, w_ready, c_in = sem("consts"), sem("w_ready"), sem("c_in")
        x_in = [sem("x_in0"), sem("x_in1")]
        bias_ready, var_ready, rstd_ready, xn_ready = (sem(n) for n in ("bias", "var", "rstd", "xn"))
        cT_psum, cT_ready, xT_psum, xT_ready = (sem(n) for n in ("cT_psum", "cT_ready", "xT_psum", "xT_ready"))
        chunk_psum, full_ready, rest_ready, second_ready, parts_ready = (
            sem(n) for n in ("chunk_psum", "full", "rest", "second", "parts"))
        parts_out = [sem(f"parts_out{r}") for r in range(RING)]
        v_psum, v_ready, v_out = sem("v_psum"), sem("v_ready"), sem("v_out")
        init_out, passed = sem("init_out"), sem("passed")
        weights = [(wq_sb, 0, q_d, 0), (wk_sb, 1, k_d, 0), (wcq_sb, 2, q_d, 1)]
        LOADS = 12
        blk = st.enter_context(nc.Block())

        def chunk(b, n):
            return KC + NCH * b + n

        def ring(n):
            return chunk(0, n) % RING

        def tile(b, t):
            return NT + NT * b + t

        def batches(eng, body):
            for u in range(2):
                body(u, u, False)
            with eng.Fori(1, B // 2 - 1, 1) as i:
                for u in range(2):
                    body(i * 2 + u, u, False)
            for u in range(2):
                body(B - 2 + u, u, u == 1)

        @blk.sync
        def _(sp):
            def load_x(b, u):
                wait(sp, xn_ready, b - 1)
                sp.dma_start(x_sb[:, u], x[bass.ds(b, 1)].rearrange("b (t p) c -> p (b t) c", p=P)).then_inc(x_in[u], 16)

            def store_parts(g, par, dst):
                sp.wait_ge(parts_ready, g + 1)
                for i in range(PARTS):
                    sp.dma_start(dst(i), parts[:, par, i, :]).then_inc(parts_out[par], 16)

            def store_values(g, dst):
                sp.wait_ge(v_ready, g + NT)
                sp.dma_start(dst.rearrange("(t p) f -> p t f", p=P), va[:].rearrange("p t h f -> p t (h f)")).then_inc(v_out, 16)

            load_x(0, 0)
            for w, d in ((Wck, wck_sb), (Wcv, wcv_sb)):
                sp.dma_start(d[:], w).then_inc(w_ready, 16)
            for w, d in ((Wq, wq_sb), (Wk, wk_sb), (Wcq, wcq_sb), (Wv, wv_sb)):
                sp.dma_start(d[:], w.rearrange("(c p) n -> p c n", p=P)).then_inc(w_ready, 16)
            with nc.allow_non_contiguous_dma(reason="biases by channel"):
                for i, b_ in enumerate((bq, bk, bcq, bck)):
                    sp.dma_start(bias[:, i, :], b_.rearrange("(c p) -> p c", p=P)).then_inc(w_ready, 16)
            for b_, d in ((bv, bv_sb), (bcv, bcv_sb)):
                sp.dma_start(d[:], b_.rearrange("(a c) -> a c", a=1).to_broadcast([P, C])).then_inc(w_ready, 16)
            load_x(1, 1)
            for g in range(KC):
                store_parts(g, g, lambda i: ck_d[i * D:(i + 1) * D, g * (H // KC):(g + 1) * (H // KC), :].rearrange("d h n -> h d n"))
            store_values(0, cv_d)

            def batch(b, u, last):
                for n in range(NCH):
                    (dst, which), oc = weights[n // KC][2:], n % KC
                    rows = dst[bass.ds(b, 1), :, which, oc * (H // KC) * S:(oc + 1) * (H // KC) * S]
                    store_parts(chunk(b, n), ring(n), lambda i: rows[:, i * D:(i + 1) * D].rearrange("b d (h n) -> (b h) d n", n=S))
                    if n == 3 and not (last or (isinstance(b, int) and b >= B - 2)):
                        load_x(b + 2, u)
                store_values(tile(b, 0), v_d[bass.ds(b, 1)].rearrange("b n f -> (b n) f"))

            batches(sp, batch)
            for par in range(RING):
                sp.wait_ge(parts_out[par], 16 * PARTS * len(range(par, chunk(B, 0), RING)))
            sp.wait_ge(v_out, 16 * (B + 1))

        @blk.gpsimd
        def _(pool):
            pool.memset(ident[:], 0.0)
            pool.memset(power[:], -0.5)
            pool.memset(zero[:], 0.0)
            pool.memset(va[:], 1.0)
            pool.memset(ids[:], 0)
            pool.drain()
            pool.affine_select(out=ident[:], in_=ident[:], compare_op=ALU.not_equal, fill=1.0, base=0,
                               pattern=[[-1, P]], channel_multiplier=1)
            pool.iota(ids[:, :, 0], pattern=[[0, E]], base=N, channel_multiplier=1)
            pool.drain()
            pool.tensor_copy(identb[:], ident[:]).then_inc(consts, 1)
            pool.wait_ge(consts, 1)
            pool.dma_start(xn_d[N:N + P, :], zero[:]).then_inc(init_out, 16)
            pool.dma_start(out[N:N + P, :], zero[:]).then_inc(init_out, 16)
            pool.dma_start(tab_d.rearrange("(p e) t -> p (e t)", p=P), ids[:].rearrange("p e t -> p (e t)")).then_inc(init_out, 16)

            def deviations(b):
                pool.wait_ge(var_ready, b + 1)
                pool.tensor_tensor(rstd[:], base[:], power[:], ALU.pow).then_inc(rstd_ready, 1)

            deviations(0)
            pool.drain()
            pool.memset(maskb[:], 0.0)
            pool.drain()
            pool.memset(cvs[:], 0.0)
            pool.drain()
            pool.memset(ks[KQ:P], 1.0)
            pool.drain()
            pool.memset(cks[KQ:P], 1.0)
            pool.drain()
            pool.affine_select(out=maskb[:], in_=maskb[:], compare_op=ALU.is_ge, fill=LOW, base=0,
                               pattern=[[-1, P]], channel_multiplier=1)
            with pool.Fori(1, B, 1) as b:
                deviations(b)
            pool.wait_ge(init_out, 48)

        @blk.tensor
        def _(pe):
            def transposes(b, u):
                pe.wait_ge(xn_ready, b + 1)
                wait(pe, xT_ready, b)
                for c in range(KC):
                    for t in range(NT):
                        mm = pe.transpose(ps[:, c, t * P:(t + 1) * P], xn_sb[:, u, t, c * P:(c + 1) * P], ident[:])
                mm.then_inc(xT_psum, 1)

            pe.wait_ge(consts, 1)
            pe.wait_ge(c_in, 16)
            for t in range(NT):
                mm = pe.transpose(ps[:, 6, t * P:(t + 1) * P], cx[:, t, :], ident[:])
            mm.then_inc(cT_psum, 1)
            transposes(0, 0)
            pe.wait_ge(cT_ready, 1)
            pe.wait_ge(w_ready, 16 * LOADS)
            for oc in range(KC):
                pe.matmul(ps[:, 2 + oc, :], wck_sb[:, oc * P:(oc + 1) * P], cxT[:], start=True, stop=True).then_inc(chunk_psum, 1)
            for t in range(NT):
                wait(pe, v_ready, t - 1)
                pe.matmul(ps[:, 6 + t % 2, 0:C], cxT[:, t * P:(t + 1) * P], wcv_sb[:], start=True, stop=True).then_inc(v_psum, 1)

            def batch(b, u, last):
                pe.wait_ge(xT_ready, b + 1)
                for n in range(NCH):
                    w, oc = weights[n // KC][0], n % KC
                    g = chunk(b, n)
                    bank = 2 + chunk(u, n) % U
                    wait(pe, full_ready, g - 3)
                    for c in range(KC):
                        mm = pe.matmul(ps[:, bank, :], w[:, c, oc * P:(oc + 1) * P], xT[:, u, c, :],
                                       start=(c == 0), stop=(c == KC - 1))
                    mm.then_inc(chunk_psum, 1)
                if not last:
                    transposes(b + 1, 1 - u)
                for t in range(NT):
                    wait(pe, v_ready, tile(b, t) - 1)
                    for c in range(KC):
                        mm = pe.matmul(ps[:, 6 + t % 2, 0:C], xT[:, u, c, t * P:(t + 1) * P], wv_sb[:, c, :],
                                       start=(c == 0), stop=(c == KC - 1))
                    mm.then_inc(v_psum, 1)

            batches(pe, batch)

        @blk.scalar
        def _(act):
            def copy_x(b, u):
                act.wait_ge(xT_psum, b + 1)
                wait(act, v_psum, tile(b, 0) - NT)
                act.copy(xT[:, u, 0, :], ps[:, 0, :])
                act.copy(xT[:, u, 1, :], ps[:, 1, :]).then_inc(xT_ready, 1)

            def copy_chunk(g, par, bank, kind, oc):
                act.wait_ge(chunk_psum, g + 1)
                wait(act, parts_ready, g - RING + 1)
                wait(act, parts_out[par], 16 * PARTS // RING * (g - par))
                scale = SCALE if kind in (0, 2) else 1.0
                act.activation(parts[:, par, 0], ps[:, bank, :], ACT.Identity, bias=scaled[:, kind, oc:oc + 1], scale=scale)
                act.activation(full[:, par], ps[:, bank, :], ACT.Identity, bias=scaled[:, kind, oc:oc + 1],
                               scale=scale).then_inc(full_ready, 1)

            def second_part(g, par):
                act.wait_ge(rest_ready, g + 1)
                act.copy(parts[:, par, 1], rest[:, par]).then_inc(second_ready, 1)

            act.dma_start(cx[:], ctx.rearrange("b k c -> (b k) c").rearrange("(t p) c -> p t c", p=P)).then_inc(c_in, 16)
            act.wait_ge(cT_psum, 1)
            act.copy(cxT[:], ps[:, 6, :]).then_inc(cT_ready, 1)
            copy_x(0, 0)
            act.wait_ge(bias_ready, 1)
            for g in range(KC):
                copy_chunk(g, g, 2 + g, 3, g)
            for g in range(KC):
                second_part(g, g)

            def batch(b, u, last):
                for n in range(NCH):
                    copy_chunk(chunk(b, n), ring(n), 2 + chunk(u, n) % U, weights[n // KC][1], n % KC)
                    if n > 0:
                        second_part(chunk(b, n - 1), ring(n - 1))
                second_part(chunk(b, NCH - 1), ring(NCH - 1))
                if not last:
                    copy_x(b + 1, 1 - u)

            batches(act, batch)

        @blk.vector
        def _(dve):
            def variances(b, u):
                dve.wait_ge(x_in[u], 8 * (b - u) + 16)
                for t in range(NT):
                    dve.bn_stats(stats[:, t], x_sb[:, u, t])
                dve.drain()
                for t in range(NT):
                    dve.bn_aggr(mv[:, t], stats[:, t])
                dve.drain()
                dve.tensor_scalar(base[:], mv[:, :, 1], EPS, None, ALU.add).then_inc(var_ready, 1)

            def normalise(b, u):
                dve.wait_ge(rstd_ready, b + 1)
                wait(dve, xT_psum, b - 1)
                for t in range(NT):
                    last = dve.tensor_scalar(xn_sb[:, u, t], x_sb[:, u, t], mv[:, t, 0:1], rstd[:, t:t + 1],
                                             ALU.subtract, ALU.mult)
                last.then_inc(xn_ready, 1)
                dve.drain()

            def subtract_first(g, par):
                dve.wait_ge(full_ready, g + 1)
                dve.tensor_tensor(rest[:, par], full[:, par], parts[:, par, 0], ALU.subtract).then_inc(rest_ready, 1)

            def third_part(g, par):
                dve.wait_ge(second_ready, g + 1)
                dve.tensor_tensor(parts[:, par, 2], rest[:, par], parts[:, par, 1], ALU.subtract).then_inc(parts_ready, 1)

            def values(done, t, b_sb):
                dve.wait_ge(v_psum, done * NT + t + 1)
                if t == 0:
                    wait(dve, v_out, 16 * done)
                dve.tensor_tensor(va[:, t, :, 0:D], ps[:, 6 + t % 2, 0:C].rearrange("p (h d) -> p h d", d=D),
                                  b_sb[:].rearrange("p (h d) -> p h d", d=D), ALU.add).then_inc(v_ready, 1)

            variances(0, 0)
            normalise(0, 0)
            dve.wait_ge(w_ready, 16 * LOADS)
            dve.tensor_copy(scaled[:], bias[:])
            dve.drain()
            dve.tensor_scalar(scaled[:, 0], bias[:, 0], SCALE, None, ALU.mult)
            dve.tensor_scalar(scaled[:, 2], bias[:, 2], SCALE, None, ALU.mult).then_inc(bias_ready, 1)
            dve.wait_ge(consts, 1)
            for g in range(KC):
                subtract_first(g, g)
            for g in range(KC):
                third_part(g, g)
            for t in range(NT):
                values(0, t, bcv_sb)

            def batch(b, u, last):
                for n in range(NCH):
                    subtract_first(chunk(b, n), ring(n))
                    if n > 0:
                        third_part(chunk(b, n - 1), ring(n - 1))
                    if n == 0 and not last:
                        variances(b + 1, 1 - u)
                    if n == 2 and not last:
                        normalise(b + 1, 1 - u)
                third_part(chunk(b, NCH - 1), ring(NCH - 1))
                for t in range(NT):
                    values(b + 1, t, bv_sb)

            batches(dve, batch)


def attend(nc, ps, ident, identb, ks, cks, cvs, maskb, q_d, k_d, ck_d, v_d, cv_d, y_d, w1, w2, w1_sb, w2_sb, w_in):
    TOTAL = B * U
    QK_LOADS = 6
    with ExitStack() as st:
        def sb(name, shape, dt):
            return st.enter_context(nc.sbuf_tensor(name, shape, dt))

        def sem(name):
            return st.enter_context(nc.semaphore("a_" + name))

        qs = sb("qs", [P, U, 2, G, S], BF16)
        ck_all = sb("ck_all", [P, H, B * SC], BF16)
        vs = sb("vs", [P, U, NT, G * HD], F32)
        negm = sb("negm", [P, 2 * G * NT], F32)
        mrest = sb("mrest", [P, 2 * G * NT], F32)
        mparts = sb("mparts", [P, PARTS, 2 * G * NT], BF16)
        mT = sb("mT", [PARTS * 2 * G * NT, P], BF16)
        pt = sb("pt", [P, 2, G, PW], F32)
        ptc = sb("ptc", [P, 2, 2, S], F32)
        o_sb = sb("o_sb", [P, 2, S], F32)
        recip = sb("recip", [P, 2, NT * G], F32)
        y2 = sb("y2", [P, 2, NT * G, D], F32)
        y_sb = sb("y_sb", [P, 2, NT, G * D], F32)

        passed = sem("passed")
        qk_in = [sem(f"qk_in{r}") for r in range(U)]
        v_in = [sem(f"v_in{r}") for r in range(U)]
        m_in = [sem("m_in0"), sem("m_in1")]
        y_out = [sem("y_out0"), sem("y_out1")]
        a_psum, a_max, m_split, mT_psum, mT_ready = (sem(n) for n in ("a_psum", "a_max", "m_split", "mT_psum", "mT_ready"))
        ck_in, ck_ready = sem("ck_in"), sem("ck_ready")
        b_psum, b_exp, masked = (sem(n) for n in ("b_psum", "b_exp", "masked"))
        o_psum, o_copied, oT_psum, y_ready = (sem(n) for n in ("o_psum", "o_copied", "oT_psum", "y_ready"))
        blk = st.enter_context(nc.Block())

        @blk.sync
        def _(sp):
            def load_qk(a):
                wait(sp, b_psum, NB * (a.s - U))
                heads = slice(a.u * G * S, (a.u + 1) * G * S)
                row = 0
                for n in (3, 2, 1):
                    rows = slice(row, row + n * D)
                    sp.dma_start(qs[rows, a.u].rearrange("p s h n -> p s (h n)"),
                                 q_d[bass.ds(a.b, 1), 0:n * D, :, heads].rearrange("b r s n -> (b r) s n")).then_inc(qk_in[a.u], 16)
                    part = 3 - n
                    sp.dma_start(ks[rows, a.u, 0].rearrange("p h n -> p (h n)"),
                                 k_d[bass.ds(a.b, 1), part * D:(part + 1) * D, 0, heads].to_broadcast([n, D, G * S])
                                 ).then_inc(qk_in[a.u], 16)
                    row += n * D

            def load_v(a):
                wait(sp, o_psum, a.s - U)
                sp.dma_start(vs[:, a.u], v_d[bass.ds(a.b, 1), :, a.u * G * HD:(a.u + 1) * G * HD].rearrange("b (t p) f -> p (b t) f", p=P)).then_inc(v_in[a.u], 16)
                for half in range(2):
                    src = cv_d[bass.ds(a.b * SC, SC), a.u * G * HD:(a.u + 1) * G * HD].rearrange("k (r f) -> k r f", f=2 * HD)
                    sp.dma_start(cvs[half * SC:(half + 1) * SC, a.u, :, half * HD:(half + 1) * HD],
                                 src[:, :, half * HD:(half + 1) * HD]).then_inc(v_in[a.u], 16)

            def load_m(a):
                sp.wait_ge(mT_ready, a.s)
                sp.dma_start(qs[KQ:KM, a.u].rearrange("p s h n -> p (s h n)"), mT[:]).then_inc(m_in[a.u % 2], 16)

            def store_y(a):
                sp.wait_ge(y_ready, a.s)
                sp.dma_start(y_d[bass.ds(a.b, 1), a.u].rearrange("b (t p) f -> p (b t) f", p=P), y_sb[:, a.u % 2]
                             ).then_inc(y_out[a.u % 2], 16)

            def step(a):
                if a.back(-1).exists:
                    load_qk(a.back(-1))
                if a.back(1).exists:
                    load_m(a.back(1))
                if a.exists:
                    load_v(a)
                if a.back(3).exists:
                    store_y(a.back(3))
                if isinstance(a.s, int) and a.s > TOTAL - U and a.exists:
                    load_expert(sp, w1, w2, w1_sb, w2_sb, w_in, a.u, a.u)

            load_qk(At(0, 0, TOTAL))
            for i, part in enumerate(KPARTS):
                sp.dma_start(ck_all[i * D:(i + 1) * D].rearrange("p h n -> p (h n)"),
                             ck_d[part * D:(part + 1) * D].rearrange("d h n -> d (h n)")).then_inc(ck_in, 16)
            steps(sp, TOTAL, 3, step)
            for par in range(2):
                sp.wait_ge(y_out[par], 8 * TOTAL)

        @blk.gpsimd
        def _(pool):
            def copy_ck(a):
                wait(pool, b_psum, NB * (a.s - U))
                pool.tensor_copy(cks[0:KQ, a.u], ck_all[0:KQ, a.u * G:(a.u + 1) * G, bass.ds(a.b * SC, SC)]).then_inc(ck_ready, 1)

            pool.wait_ge(ck_in, 16 * len(KPARTS))
            copy_ck(At(0, 0, TOTAL))

            def step(a):
                if a.back(-1).exists:
                    copy_ck(a.back(-1))
                x = a.back(2)
                if x.exists:
                    wait_apart(pool, b_exp, NB * (x.s - 1) + NB - 1, passed)
                    for j in range(NT):
                        block = pt[:, x.u % 2, :, OFF[j]:OFF[j] + P]
                        pool.affine_select(out=block, in_=block, compare_op=ALU.is_ge, fill=0.0, base=0,
                                           pattern=[[0, G], [1, P]], channel_multiplier=-1).then_inc(masked, 1)

            steps(pool, TOTAL, 3, step)

        @blk.tensor
        def _(pe):
            def scores_by_query(a, k):
                g = NA * (a.s - 1) + k
                bank = (NA * a.u + k) % 2
                wait(pe, a_max, g - 1)
                if k < 11:
                    t = 0 if k < 1 else 1 if k < 3 else 2 if k < 7 else 3
                    first, count = ((0, 4), (0, 2), (2, 2), *((h, 1) for h in range(4)), *((h, 1) for h in range(4)))[k]
                    w = P * (t + 1)
                    for i in range(count):
                        h = first + i
                        pe.matmul(ps[:, bank, i * w:(i + 1) * w], qs[0:KQ, a.u, 0, h, t * P:(t + 1) * P], ks[0:KQ, a.u, 0, h, 0:w],
                                  start=True, stop=False)
                        mm = pe.matmul(ps[:, bank, i * w + t * P:(i + 1) * w], identb[:], maskb[:], start=False, stop=True)
                else:
                    if k == 11:
                        pe.wait_ge(ck_ready, a.s)
                    for i in range(2):
                        t = 2 * (k - 11) + i
                        for h in range(G):
                            at = (i * G + h) * SC
                            mm = pe.matmul(ps[:, bank, at:at + SC], qs[0:KQ, a.u, 1, h, t * P:(t + 1) * P], cks[0:KQ, a.u, h, :],
                                           start=True, stop=True)
                mm.then_inc(a_psum, 1)

            def maxima_to_rows(a):
                pe.wait_ge(m_split, a.s)
                wait(pe, y_ready, a.s - 3)
                pe.transpose(ps[0:mT.shape[0], 7, 0:P // 2].bitcast(BF16), mparts[:].rearrange("p i m -> p (i m)"), identb[:]
                             ).then_inc(mT_psum, 1)

            def scores_by_key(a, k):
                g = NB * (a.s - 1) + k
                bank = 2 + 2 * ((NB * a.u + k) % 2)
                wait(pe, b_exp, g - 1)
                if k == 0:
                    pe.wait_ge(m_in[a.u % 2], a.uses(2, 16) + 16)
                if k == 6:
                    for h in range(G):
                        r = (h % 2) * SC
                        mm = pe.matmul(ps[r:r + SC, bank + h // 2, :], cks[0:KM, a.u, h, :], qs[0:KM, a.u, 1, h, :],
                                       start=True, stop=True)
                else:
                    todo = [(2 * (k // 3) + k % 3, j, j, 0) for j in (0, 1)] if k % 3 < 2 else \
                        [(2 * (k // 3) + i, j, i, OFF[j] - OFF[2]) for i in (0, 1) for j in (2, 3)]
                    for h, j, bk_, at in todo:
                        mm = pe.matmul(ps[:, bank + bk_, at:at + WID[j]], ks[0:KM, a.u, 0, h, j * P:(j + 1) * P],
                                       qs[0:KM, a.u, 0, h, j * P:S], start=True, stop=True)
                mm.then_inc(b_psum, 1)

            def outputs(a, j):
                if j == 0:
                    wait(pe, y_ready, a.s - 1)
                    pe.wait_ge(masked, NT * a.s)
                    pe.wait_ge(v_in[a.u], a.uses(4, 48) + 48)
                for h in range(G):
                    pe.matmul(ps[h * HD:(h + 1) * HD, 6, j * P:S], vs[:, a.u, j, h * HD:(h + 1) * HD],
                              pt[:, a.u % 2, h, OFF[j]:OFF[j] + WID[j]], start=(j == 0), stop=(j == NT - 1))

            def cross_outputs(a):
                pe.wait_ge(b_exp, NB * a.s)
                if a.back(-2).exists:
                    pe.wait_ge(mT_ready, a.s + 2)
                for r in range(2):
                    mm = pe.matmul(ps[r * SC:(r + 1) * SC, 7, :], cvs[:, a.u, r, :], ptc[:, a.u % 2, r, :], start=True, stop=True)
                mm.then_inc(o_psum, 1)

            def outputs_by_token(a):
                pe.wait_ge(o_copied, a.s)
                for i in range(2):
                    for t in range(NT):
                        mm = pe.transpose(ps[:, 6 + i, t * P:(t + 1) * P], o_sb[:, i, t * P:(t + 1) * P], ident[:])
                mm.then_inc(oT_psum, 1)

            def step(a):
                m, b, o = a.back(1), a.back(2), a.back(3)

                def A(*ks_):
                    for k in ks_:
                        if a.exists:
                            if k == 0:
                                pe.wait_ge(qk_in[a.u], a.uses(4, 16 * QK_LOADS) + 16 * QK_LOADS)
                            scores_by_query(a, k)

                def BK(k):
                    if b.exists:
                        scores_by_key(b, k)

                def CO(j):
                    if o.exists:
                        outputs(o, j)

                A(0, 1)
                CO(0)
                BK(0)
                if m.exists:
                    maxima_to_rows(m)
                A(2, 3)
                BK(1)
                CO(1)
                A(4, 5)
                BK(2)
                CO(2)
                A(6, 7)
                BK(3)
                CO(3)
                if o.exists:
                    cross_outputs(o)
                A(8)
                BK(4)
                A(9, 10)
                if o.exists:
                    outputs_by_token(o)
                BK(5)
                A(11, 12)
                BK(6)

            steps(pe, TOTAL, 3, step)

        @blk.scalar
        def _(act):
            def exponentials(a, k):
                bank = 2 + 2 * ((NB * a.u + k) % 2)
                act.wait_ge(b_psum, NB * (a.s - 1) + k + 1)
                if k == 0:
                    wait(act, o_psum, a.s - 2)
                two = ps[:, bank:bank + 2, :]
                if k == 6:
                    src, dst = two, ptc[:, a.u % 2]
                elif k % 3 < 2:
                    w = WID[0] + WID[1]
                    src, dst = two.rearrange("p b n -> p (b n)")[:, 0:w], pt[:, a.u % 2, 2 * (k // 3) + k % 3, 0:w]
                else:
                    src, dst = two[:, :, 0:PW - OFF[2]], pt[:, a.u % 2, 2 * (k // 3):2 * (k // 3) + 2, OFF[2]:PW]
                act.activation(dst, src, ACT.Exp).then_inc(b_exp, 1)

            def step(a):
                b, o = a.back(2), a.back(3)
                for k in range(NB):
                    if b.exists:
                        exponentials(b, k)
                    if k == 3 and o.exists:
                        act.wait_ge(o_psum, o.s)
                        wait(act, oT_psum, o.s - 1)
                        act.copy(o_sb[:, 0], ps[:, 6, :])
                        act.copy(o_sb[:, 1], ps[:, 7, :]).then_inc(o_copied, 1)

            steps(act, TOTAL, 3, step)

        @blk.vector
        def _(dve):
            def maxima(a, k):
                bank = (NA * a.u + k) % 2
                dve.wait_ge(a_psum, NA * (a.s - 1) + k + 1)
                if k == 0:
                    dst, src = negm[:, 0:G * NT:NT], ps[:, bank, :].rearrange("p (h n) -> p h n", h=G)
                elif k < 3:
                    lo = 2 * (k - 1) * NT + 1
                    dst, src = negm[:, lo:lo + NT + 1:NT], ps[:, bank, :].rearrange("p (h n) -> p h n", h=2)
                elif k < 11:
                    h, t = (k - 3) % 4, 2 + (k - 3) // 4
                    dst, src = negm[:, h * NT + t:h * NT + t + 1], ps[:, bank, 0:(t + 1) * P]
                else:
                    t = 2 * (k - 11)
                    dst = negm[:, G * NT:].rearrange("p (h t) -> p t h", t=NT)[:, t:t + 2, :]
                    src = ps[:, bank, :].rearrange("p (t h n) -> p t h n", t=2, h=G)
                dve.tensor_reduce(dst, src, AX.X, ALU.max, negate=True).then_inc(a_max, 1)

            def split_maxima(a):
                dve.drain()
                dve.tensor_copy(mparts[:, 0], negm[:])
                dve.drain()
                dve.tensor_tensor(mrest[:], negm[:], mparts[:, 0], ALU.subtract)
                dve.drain()
                dve.tensor_copy(mparts[:, 1], mrest[:])
                dve.drain()
                dve.tensor_tensor(mparts[:, 2], mrest[:], mparts[:, 1], ALU.subtract).then_inc(m_split, 1)
                dve.drain()

            def copy_maxima(a):
                dve.wait_ge(mT_psum, a.s)
                if a.back(1).exists:
                    x = a.back(1)
                    wait(dve, m_in[x.u % 2], x.uses(2, 16) + 16)
                dve.tensor_copy(mT[:], ps[0:mT.shape[0], 7, 0:P // 2].bitcast(BF16)).then_inc(mT_ready, 1)

            def normalise(a):
                dve.wait_ge(oT_psum, a.s)
                wait(dve, y_out[a.u % 2], a.uses(2, 16))
                for i in range(2):
                    heads = ps[:, 6 + i, :].rearrange("p (x f) -> p x f", f=HD)
                    dve.reciprocal(recip[:, i].rearrange("p (x o) -> p x o", o=1), heads[:, :, D:D + 1])
                dve.drain()
                for i in range(2):
                    heads = ps[:, 6 + i, :].rearrange("p (x f) -> p x f", f=HD)
                    dve.tensor_tensor(y2[:, i], heads[:, :, 0:D],
                                      recip[:, i].rearrange("p (x o) -> p x o", o=1).to_broadcast([P, NT * G, D]), ALU.mult)
                dve.drain()
                dve.tensor_tensor(y_sb[:, a.u % 2].rearrange("p t f -> p (t f)"), y2[:, 0].rearrange("p x d -> p (x d)"),
                                  y2[:, 1].rearrange("p x d -> p (x d)"), ALU.add).then_inc(y_ready, 1)
                dve.drain()

            def step(a):
                m, o = a.back(1), a.back(3)
                for k in range(NA):
                    if a.exists:
                        maxima(a, k)
                    if k == 1 and m.exists:
                        copy_maxima(m)
                    if k == 10 and o.exists:
                        normalise(o)
                if a.exists:
                    split_maxima(a)

            steps(dve, TOTAL, 3, step)


def route(nc, ps, ident, x, Wp, bp, gate_w, gate_b, b2, y_d, xn_d, tab_d, b2_d, out):
    TOTAL = N // P
    with ExitStack() as st:
        def sb(name, shape, dt):
            return st.enter_context(nc.sbuf_tensor(name, shape, dt))

        def sem(name):
            return st.enter_context(nc.semaphore("r_" + name))

        wp_sb = sb("wp_sb", [P, KC, C], F32)
        gw_sb = sb("gw_sb", [P, KC, E], F32)
        bp_sb = sb("bp_sb", [1, C], F32)
        one = sb("one", [1, P], F32)
        gb_sb = sb("gb_sb", [P, E], F32)
        b2_sb, b2_rest = sb("b2_sb", [E, C], F32), sb("b2_rest", [E, C], F32)
        b2_parts = sb("b2_parts_sb", [E, PARTS, C], BF16)
        before = sb("before", [P, P], BF16)
        ones = sb("ones", [P, P], BF16)
        expert = sb("expert", [P, E], F32)
        token = sb("token", [P, 1], F32)
        y_in = sb("y_in_sb", [P, U, U, G * D], F32)
        x_in_sb = sb("x_in_sb", [P, U, C], F32)
        yT = sb("yT", [P, U, KC, P], F32)
        x1 = sb("x1", [P, U, C], F32)
        stats, mv = sb("r_stats", [P, 6], F32), sb("r_mv", [P, U, 2], F32)
        base, rstd, power = sb("r_base", [P, U], F32), sb("r_rstd", [P, U], F32), sb("r_power", [P, 1], F32)
        xn = sb("xn", [P, U, C], F32)
        xnT = sb("xnT", [P, U, KC, P], F32)
        lg = sb("lg", [P, U, E], F32)
        top = sb("top", [P, U, 8], F32)
        top_i = sb("top_i", [P, U, 8], U32)
        neg_top = sb("neg_top", [P, U], F32)
        hot = sb("hot", [P, U, TOPK, E], F32)
        chosen = sb("chosen", [P, U, E], BF16)
        sofar = sb("sofar", [P, U, E], BF16)
        picked = sb("picked", [P, TOPK, E], F32)
        place = sb("place", [P, TOPK], F32)
        slot = sb("slot", [P, U, TOPK], U32)
        eg = sb("eg", [P, U, TOPK], F32)
        esum = sb("esum", [P, U], F32)
        einv = sb("einv", [P, 1], F32)
        row = sb("row", [P, U, TOPK, 2], I32)

        consts, w_ready, passed = sem("consts"), sem("w_ready"), sem("passed")
        b2_ready, b2_out = sem("b2_ready"), sem("b2_out")
        loaded = [sem(f"loaded{r}") for r in range(U)]
        x1_out = [sem(f"x1_out{r}") for r in range(U)]
        table_out = [sem(f"table_out{r}") for r in range(U)]
        yT_psum, yT_ready, p_psum, x1_ready = (sem(n) for n in ("yT_psum", "yT_ready", "p_psum", "x1"))
        var_ready, rstd_ready, xn_ready, xnT_psum, xnT_ready = (sem(n) for n in ("var", "rstd", "xn", "xnT_psum", "xnT_ready"))
        lg_psum, top_ready, hot_ready, exp_ready, place_psum, row_ready = (
            sem(n) for n in ("lg_psum", "top", "hot", "exp", "place_psum", "row"))
        LOADS = 4
        blk = st.enter_context(nc.Block())

        @blk.sync
        def _(sp):
            sp.dma_start(wp_sb[:], Wp.rearrange("(c p) n -> p c n", p=P)).then_inc(w_ready, 16)
            sp.dma_start(bp_sb[:], bp.rearrange("(a c) -> a c", a=1)).then_inc(w_ready, 16)
            sp.dma_start(gw_sb[:], gate_w.rearrange("(c p) n -> p c n", p=P)).then_inc(w_ready, 16)
            sp.dma_start(gb_sb[:], gate_b.rearrange("(a c) -> a c", a=1).to_broadcast([P, E])).then_inc(w_ready, 16)

            def load(a):
                wait(sp, yT_psum, a.s - U)
                wait(sp, x1_ready, a.s - U)
                sp.dma_start(y_in[:, a.u], y_d[bass.ds(a.b, 1), :, a.u * P:(a.u + 1) * P, :].rearrange("b g t f -> t (b g) f")
                             ).then_inc(loaded[a.u], 16)
                sp.dma_start(x_in_sb[:, a.u], x[bass.ds(a.b, 1), a.u * P:(a.u + 1) * P, :].rearrange("b t c -> (b t) c")
                             ).then_inc(loaded[a.u], 16)

            def store(a):
                sp.wait_ge(xn_ready, a.s)
                sp.dma_start(out[bass.ds(a.b * S + a.u * P, P), :], x1[:, a.u]).then_inc(x1_out[a.u], 16)
                sp.dma_start(xn_d[bass.ds(a.b * S + a.u * P, P), :], xn[:, a.u]).then_inc(x1_out[a.u], 16)

            def step(a):
                if a.back(-3).exists:
                    load(a.back(-3))
                if a.back(1).exists:
                    store(a.back(1))

            for u in range(3):
                load(At(0, u, TOTAL))
            sp.dma_start(b2_sb[:], b2).then_inc(b2_out, 16)
            sp.wait_ge(b2_ready, 1)
            sp.dma_start(b2_d.rearrange("i e c -> e i c"), b2_parts[:]).then_inc(b2_out, 16)
            steps(sp, TOTAL, 5, step)
            sp.wait_ge(b2_out, 32)
            for r in range(U):
                sp.wait_ge(x1_out[r], 32 * (TOTAL // U))

        @blk.gpsimd
        def _(pool):
            pool.memset(before[:], 1.0)
            pool.memset(ones[:], 1.0)
            pool.memset(sofar[:], 0.0)
            pool.memset(one[:], 1.0)
            pool.memset(power[:], -0.5)
            pool.iota(expert[:], pattern=[[1, E]], base=0, channel_multiplier=0, allow_small_or_imprecise_dtypes=True)
            pool.iota(token[:], pattern=[[0, 1]], base=0, channel_multiplier=1, allow_small_or_imprecise_dtypes=True)
            pool.drain()
            pool.affine_select(out=before[:], in_=before[:], compare_op=ALU.is_gt, fill=0.0, base=0,
                               pattern=[[1, P]], channel_multiplier=-1).then_inc(consts, 1)

            def deviation(a):
                pool.wait_ge(var_ready, a.s)
                pool.tensor_tensor(rstd[:, a.u:a.u + 1], base[:, a.u:a.u + 1], power[:], ALU.pow).then_inc(rstd_ready, 1)

            def scatter(a):
                wait_apart(pool, row_ready, a.s, passed)
                for k in range(TOPK):
                    pool.indirect_dma_start(out=tab_d, out_offset=bass.IndirectOffsetOnAxis(ap=slot[:, a.u, k:k + 1], axis=0),
                                            in_=row[:, a.u, k, :], in_offset=None, bounds_check=CAP * E - 1,
                                            oob_is_err=False).then_inc(table_out[a.u], 16)

            def step(a):
                if a.back(1).exists:
                    deviation(a.back(1))
                if a.back(5).exists:
                    scatter(a.back(5))

            steps(pool, TOTAL, 5, step)
            for r in range(U):
                pool.wait_ge(table_out[r], 16 * TOPK * (TOTAL // U))

        @blk.tensor
        def _(pe):
            pe.wait_ge(w_ready, 16 * LOADS)
            pe.wait_ge(consts, 1)

            def step(a):
                if a.exists:
                    pe.wait_ge(loaded[a.u], a.uses(4, 32) + 32)
                    wait(pe, yT_ready, a.s - 1)
                    for c in range(KC):
                        mm = pe.transpose(ps[:, 0, c * P:(c + 1) * P],
                                          y_in[:, a.u].rearrange("p g f -> p (g f)")[:, c * P:(c + 1) * P], ident[:])
                    mm.then_inc(yT_psum, 1)
                x_ = a.back(1)
                if x_.exists:
                    pe.wait_ge(yT_ready, x_.s)
                    wait(pe, x1_ready, x_.s - 2)
                    pe.matmul(ps[:, 1 + 4 * (x_.u % 2), 0:C], one[:], bp_sb[:], start=True, stop=False)
                    for c in range(KC):
                        mm = pe.matmul(ps[:, 1 + 4 * (x_.u % 2), 0:C], yT[:, x_.u, c, :], wp_sb[:, c, :], start=False, stop=(c == KC - 1))
                    mm.then_inc(p_psum, 1)
                x_ = a.back(2)
                if x_.exists:
                    pe.wait_ge(xn_ready, x_.s)
                    wait(pe, xnT_ready, x_.s - 1)
                    for c in range(KC):
                        mm = pe.transpose(ps[:, 2, c * P:(c + 1) * P], xn[:, x_.u, c * P:(c + 1) * P], ident[:])
                    mm.then_inc(xnT_psum, 1)
                x_ = a.back(3)
                if x_.exists:
                    pe.wait_ge(xnT_ready, x_.s)
                    wait(pe, top_ready, x_.s - 2)
                    for c in range(KC):
                        mm = pe.matmul(ps[:, 3 + 4 * (x_.u % 2), 0:E], xnT[:, x_.u, c, :], gw_sb[:, c, :], start=(c == 0), stop=(c == KC - 1))
                    mm.then_inc(lg_psum, 1)
                x_ = a.back(4)
                if x_.exists:
                    pe.wait_ge(hot_ready, x_.s)
                    wait(pe, row_ready, x_.s - 2)
                    pe.matmul(ps[:, 4 + 2 * (x_.u % 2), 0:E], before[:], chosen[:, x_.u, :], start=True, stop=False)
                    pe.matmul(ps[:, 4 + 2 * (x_.u % 2), 0:E], ones[:], sofar[:, x_.u, :], start=False, stop=True).then_inc(place_psum, 1)

            steps(pe, TOTAL, 5, step)

        @blk.scalar
        def _(act):
            def step(a):
                if a.exists:
                    act.wait_ge(yT_psum, a.s)
                    wait(act, p_psum, a.s - U)
                    act.copy(yT[:, a.u].rearrange("p c n -> p (c n)"), ps[:, 0, 0:C]).then_inc(yT_ready, 1)
                x_ = a.back(2)
                if x_.exists:
                    act.wait_ge(xnT_psum, x_.s)
                    wait(act, lg_psum, a.s - 5)
                    act.copy(xnT[:, x_.u].rearrange("p c n -> p (c n)"), ps[:, 2, 0:C]).then_inc(xnT_ready, 1)
                x_ = a.back(3)
                if x_.exists:
                    act.wait_ge(hot_ready, x_.s)
                    wait(act, row_ready, x_.s - U)
                    act.activation(eg[:, x_.u], top[:, x_.u, 0:TOPK], ACT.Exp, bias=neg_top[:, x_.u:x_.u + 1],
                                   accum_out=esum[:, x_.u:x_.u + 1]).then_inc(exp_ready, 1)

            steps(act, TOTAL, 5, step)

        @blk.vector
        def _(dve):
            dve.wait_ge(b2_out, 16)
            dve.tensor_copy(b2_parts[:, 0], b2_sb[:])
            dve.drain()
            dve.tensor_tensor(b2_rest[:], b2_sb[:], b2_parts[:, 0], ALU.subtract)
            dve.drain()
            dve.tensor_copy(b2_parts[:, 1], b2_rest[:])
            dve.drain()
            dve.tensor_tensor(b2_parts[:, 2], b2_rest[:], b2_parts[:, 1], ALU.subtract).then_inc(b2_ready, 1)
            dve.wait_ge(w_ready, 16 * LOADS)
            dve.wait_ge(consts, 1)

            def step(a):
                r, c, f, e = (a.back(k) for k in (1, 3, 4, 5))
                if r.exists:
                    dve.wait_ge(p_psum, r.s)
                    dve.wait_ge(loaded[r.u], r.uses(4, 32) + 32)
                    wait(dve, x1_out[r.u], r.uses(4, 32))
                    dve.tensor_tensor(x1[:, r.u], ps[:, 1 + 4 * (r.u % 2), 0:C], x_in_sb[:, r.u], ALU.add).then_inc(x1_ready, 1)
                if e.exists:
                    dve.wait_ge(place_psum, e.s)
                    dve.wait_ge(exp_ready, e.s)
                    dve.tensor_tensor(picked[:], hot[:, e.u], ps[:, 4 + 2 * (e.u % 2), 0:E].rearrange("p (o e) -> p o e", o=1).to_broadcast([P, TOPK, E]),
                                      ALU.mult)
                    dve.reciprocal(einv[:], esum[:, e.u:e.u + 1])
                dve.drain()
                if r.exists:
                    dve.bn_stats(stats[:], x1[:, r.u])
                if f.exists:
                    dve.tensor_tensor(sofar[:, (f.u + 1) % U], sofar[:, f.u], chosen[:, f.u], ALU.add)
                if e.exists:
                    wait(dve, table_out[e.u], e.uses(4, 16 * TOPK))
                    dve.tensor_reduce(place[:], picked[:], AX.X, ALU.add)
                    dve.tensor_scalar(row[:, e.u, :, 1].bitcast(F32), eg[:, e.u], einv[:, 0:1], None, ALU.mult)
                    dve.tensor_copy(row[:, e.u, :, 0], token[:].to_broadcast([P, TOPK]))
                dve.drain()
                if r.exists:
                    dve.bn_aggr(mv[:, r.u], stats[:])
                if e.exists:
                    dve.tensor_scalar(token[:], token[:], float(P), None, ALU.add)
                    dve.scalar_tensor_tensor(out=slot[:, e.u], in0=place[:], scalar=float(E), in1=top_i[:, e.u, 0:TOPK],
                                             op0=ALU.mult, op1=ALU.add).then_inc(row_ready, 1)
                dve.drain()
                if r.exists:
                    dve.tensor_scalar(base[:, r.u:r.u + 1], mv[:, r.u, 1:2], EPS, None, ALU.add).then_inc(var_ready, 1)
                if c.exists:
                    dve.wait_ge(lg_psum, c.s)
                    dve.tensor_tensor(lg[:, c.u], ps[:, 3 + 4 * (c.u % 2), 0:E], gb_sb[:], ALU.add).then_inc(top_ready, 1)
                    dve.drain()
                    dve.max(top[:, c.u], lg[:, c.u])
                    dve.drain()
                    dve.max_index(top_i[:, c.u], top[:, c.u], lg[:, c.u])
                    dve.tensor_scalar(neg_top[:, c.u:c.u + 1], top[:, c.u, 0:1], -1.0, None, ALU.mult)
                    dve.drain()
                    dve.tensor_tensor(hot[:, c.u], expert[:].rearrange("p (o e) -> p o e", o=1).to_broadcast([P, TOPK, E]),
                                      top_i[:, c.u, 0:TOPK].rearrange("p (k o) -> p k o", o=1).to_broadcast([P, TOPK, E]), ALU.is_equal)
                if r.exists:
                    dve.wait_ge(rstd_ready, r.s)
                    dve.tensor_scalar(xn[:, r.u], x1[:, r.u], mv[:, r.u, 0:1], rstd[:, r.u:r.u + 1],
                                      ALU.subtract, ALU.mult).then_inc(xn_ready, 1)
                dve.drain()
                if c.exists:
                    wait(dve, place_psum, c.s - U + 1)
                    with nc.allow_low_precision(reason="counts up to three are exact"):
                        dve.tensor_reduce(chosen[:, c.u], hot[:, c.u].rearrange("p k e -> p e k"), AX.X, ALU.add).then_inc(hot_ready, 1)

            steps(dve, TOTAL, 5, step)


def experts(nc, ps, ident, w1, b1, w2, xn_d, tab_d, b2_d, out, w1_sb, w2_sb, w_in):
    with ExitStack() as st:
        def sb(name, shape, dt):
            return st.enter_context(nc.sbuf_tensor(name, shape, dt))

        def sem(name):
            return st.enter_context(nc.semaphore("e_" + name))

        tab = sb("tab", [P, E, 2], I32)
        b1_rows = sb("b1_rows", [P, E * FC // P, P], F32)
        b1T = sb("b1T", [P, E * FC], F32)
        b2p = sb("b2p", [PARTS, E * C], BF16)
        ones3 = sb("ones3", [PARTS, P], BF16)
        from_ids, to_ids = sb("from_ids", [P, U], I32), sb("to_ids", [P, U], I32)
        xg = sb("xg", [P, U, C], F32)
        xgT = sb("xgT", [P, 2, KC, P], F32)
        hT = sb("hT", [P, 2, FC, P], F32)
        yg = sb("yg", [P, U, C], F32)

        setup, tab_in, ones_ready = sem("setup"), sem("tab_in"), sem("ones")
        b1_psum, b1_ready = sem("b1_psum"), sem("b1_ready")
        ids_ready, to_ready = sem("ids"), sem("to_ready")
        gathered = [sem(f"gathered{r}") for r in range(U)]
        added, passed = sem("added"), sem("passed")
        xT_psum, xT_ready, h_psum, h_ready, y_psum, y_ready = (
            sem(n) for n in ("xT_psum", "xT_ready", "h_psum", "h_ready", "y_psum", "y_ready"))
        blk = st.enter_context(nc.Block())

        @blk.sync
        def _(sp):
            sp.dma_start(tab[:].rearrange("p e t -> p (e t)"), tab_d.rearrange("(p e) t -> p (e t)", p=P)).then_inc(tab_in, 16)
            sp.dma_start(b1_rows[:], b1.rearrange("e (c p) -> (e c) p", p=P).rearrange("(g q) p -> q g p", q=P)).then_inc(setup, 16)
            sp.dma_start(b2p[:], b2_d.rearrange("i e c -> i (e c)")).then_inc(setup, 16)

            def step(a):
                if a.exists and not (isinstance(a.s, int) and a.s <= U):
                    sp.wait_ge(y_psum, a.s - U)
                    load_expert(sp, w1, w2, w1_sb, w2_sb, w_in, a.b * U + a.u, a.u)

            steps(sp, E, 1, step)

        @blk.gpsimd
        def _(pool):
            pool.memset(ones3[:], 1.0).then_inc(ones_ready, 1)
            pool.wait_ge(tab_in, 16)

            def gather(a):
                wait(pool, xT_psum, a.s - U)
                wait_apart(pool, gathered[a.u], a.uses(4, 16), passed)
                pool.tensor_copy(from_ids[:, a.u:a.u + 1], tab[:, bass.ds(a.b * U + a.u, 1), 0]).then_inc(ids_ready, 1)
                wait_apart(pool, ids_ready, a.s, passed)
                pool.indirect_dma_start(out=xg[:, a.u], out_offset=None, in_=xn_d,
                                        in_offset=bass.IndirectOffsetOnAxis(ap=from_ids[:, a.u:a.u + 1].bitcast(U32), axis=0),
                                        bounds_check=N + P - 1).then_inc(gathered[a.u], 16)

            def add(a):
                wait_apart(pool, added, 16 * (a.s - 1), passed)
                pool.tensor_copy(to_ids[:, a.u:a.u + 1], tab[:, bass.ds(a.b * U + a.u, 1), 0]).then_inc(to_ready, 1)
                pool.wait_ge(to_ready, a.s)
                wait_apart(pool, y_ready, a.s, passed)
                pool.indirect_dma_start(out=out, out_offset=bass.IndirectOffsetOnAxis(ap=to_ids[:, a.u:a.u + 1].bitcast(U32), axis=0),
                                        in_=yg[:, a.u], in_offset=None, bounds_check=N + P - 1, compute_op=ALU.add
                                        ).then_inc(added, 16)

            def step(a):
                if a.back(-3).exists:
                    gather(a.back(-3))
                if a.back(1).exists:
                    add(a.back(1))

            for u in range(3):
                gather(At(0, u, E))
            steps(pool, E, 1, step)
            pool.wait_ge(added, 16 * E)

        @blk.tensor
        def _(pe):
            def tokens_by_channel(a):
                pe.wait_ge(gathered[a.u], a.uses(4, 16) + 16)
                wait(pe, xT_ready, a.s - 2)
                for c in range(KC):
                    mm = pe.transpose(ps[:, a.u % 2, c * P:(c + 1) * P], xg[:, a.u, c * P:(c + 1) * P], ident[:])
                mm.then_inc(xT_psum, 1)

            def first_layer(a):
                pe.wait_ge(w_in[a.u], a.uses(4, 32) + 32)
                pe.wait_ge(xT_ready, a.s)
                for n in range(FC):
                    if n % 4 == 0:
                        wait(pe, h_ready, FC * (a.s - 2))
                    for c in range(KC):
                        mm = pe.matmul(ps[:, 2 + 2 * (a.u % 2) + n // 4, (n % 4) * P:(n % 4 + 1) * P],
                                       w1_sb[:, a.u, c, n * P:(n + 1) * P], xgT[:, a.u % 2, c, :], start=(c == 0), stop=(c == KC - 1))
                    if n % 4 == 3:
                        mm.then_inc(h_psum, 1)

            def second_layer(a):
                pe.wait_ge(h_ready, FC * a.s)
                wait(pe, y_ready, a.s - 2)
                bank = ps[:, 6 + a.u % 2, 0:C]
                pe.matmul(bank, ones3[:], b2p[:, bass.ds((a.b * U + a.u) * C, C)], start=True, stop=False)
                for n in range(FC):
                    mm = pe.matmul(bank, hT[:, a.u % 2, n, :], w2_sb[:, a.u, n, :], start=False, stop=(n == FC - 1))
                mm.then_inc(y_psum, 1)

            pe.wait_ge(setup, 32)
            pe.wait_ge(ones_ready, 1)
            for g in range(E * FC // P):
                mm = pe.transpose(ps[:, 7, g * P:(g + 1) * P], b1_rows[:, g, :], ident[:])
            mm.then_inc(b1_psum, 1)
            tokens_by_channel(At(0, 0, E))
            pe.wait_ge(b1_ready, 1)

            def step(a):
                if a.back(-1).exists:
                    tokens_by_channel(a.back(-1))
                if a.exists:
                    first_layer(a)
                if a.back(1).exists:
                    second_layer(a.back(1))

            steps(pe, E, 1, step)

        @blk.scalar
        def _(act):
            act.wait_ge(b1_psum, 1)
            act.copy(b1T[:], ps[:, 7, :]).then_inc(b1_ready, 1)
            act.wait_ge(b1_ready, 1)

            def step(a):
                if a.exists:
                    for n in range(FC):
                        if n % 4 == 0:
                            act.wait_ge(h_psum, FC // 4 * (a.s - 1) + n // 4 + 1)
                        if n == 0:
                            wait(act, y_psum, a.s - 2)
                        act.activation(hT[:, a.u % 2, n, :], ps[:, 2 + 2 * (a.u % 2) + n // 4, (n % 4) * P:(n % 4 + 1) * P],
                                       ACT.Gelu, bias=b1T[:, bass.ds((a.b * U + a.u) * FC + n, 1)]).then_inc(h_ready, 1)

            steps(act, E, 1, step)

        @blk.vector
        def _(dve):
            dve.wait_ge(tab_in, 16)

            def copy_tokens(a):
                dve.wait_ge(xT_psum, a.s)
                wait(dve, h_psum, FC // 4 * (a.s - 2))
                dve.tensor_copy(xgT[:, a.u % 2].rearrange("p c n -> p (c n)"), ps[:, a.u % 2, 0:C]).then_inc(xT_ready, 1)

            def scale_rows(a):
                dve.wait_ge(y_psum, a.s)
                wait(dve, added, 16 * (a.s - U))
                dve.tensor_scalar(yg[:, a.u], ps[:, 6 + a.u % 2, 0:C],
                                  tab[:, bass.ds(a.b * U + a.u, 1), 1].bitcast(F32), None, ALU.mult).then_inc(y_ready, 1)

            copy_tokens(At(0, 0, E))

            def step(a):
                if a.back(-1).exists:
                    copy_tokens(a.back(-1))
                if a.back(1).exists:
                    scale_rows(a.back(1))

            steps(dve, E, 1, step)


_INS = ["x", "ctx_512", "L0_xattn_Wk", "L0_xattn_bk", "L0_xattn_Wq", "L0_xattn_bq", "L0_xattn_Wv", "L0_xattn_bv",
        "L0_xattn_Wck", "L0_xattn_bck", "L0_xattn_Wcq", "L0_xattn_bcq", "L0_xattn_Wcv", "L0_xattn_bcv",
        "L0_xattn_Wp", "L0_xattn_bp", "L0_ffn_gate_w", "L0_ffn_gate_b", "L0_ffn_w1", "L0_ffn_b1", "L0_ffn_w2", "L0_ffn_b2"]


def kernel(**inputs):
    import numpy as np
    import concourse.bacc as bacc
    from concourse.bass_utils import run_bass_kernel_spmd

    nc = bacc.Bacc("TRN2", target_bir_lowering=False, num_devices=1)
    arrays, args = {}, []
    for name in _INS:
        a = np.ascontiguousarray(inputs[name])
        arrays[f"in_{name}"] = a
        args.append(nc.dram_tensor(f"in_{name}", a.shape, mybir.dt.from_np(a.dtype), kind="ExternalInput").ap())
    out = nc.dram_tensor("out_rows", (N + P, C), F32, kind="ExternalOutput").ap()
    layer_kernel(nc, *args, out)
    r = run_bass_kernel_spmd(nc, [arrays], core_ids=[0])
    return r.results[0]["out_rows"][:N].reshape(B, S, C)
```

```python
from contextlib import ExitStack

import concourse.bass as bass
from concourse import mybir

ALU = mybir.AluOpType
ACT = mybir.ActivationFunctionType
AX = mybir.AxisListType
F32 = mybir.dt.float32
F32R = mybir.dt.float32r
BF16 = mybir.dt.bfloat16
I32 = mybir.dt.int32
U32 = mybir.dt.uint32

P = 128
B, S, C = 8, 512, 256
CC, SC = 128, 64
H, D = 16, 16
G = 4
U = H // G
NT = S // P
KC = C // P
N = B * S
E, TOPK, CAP, F = 64, 3, 128, 1024
FC = F // P
BP, GB, ROWS = E, E + 1, E + 2
EPS = 1e-5
PARTS = 3
KPARTS = (0, 0, 0, 1, 1, 2)
KQ = len(KPARTS) * D
KM = KQ + PARTS
HD = 32
WID = [S - P * j for j in range(NT)]
OFF = [sum(WID[:j]) for j in range(NT)]
PW = sum(WID)
NA, NB = 13, 7
SCALE = D ** -0.5
LOW = -1e30


def wait(eng, sem, value):
    if not isinstance(value, int) or value > 0:
        eng.wait_ge(sem, value)


def wait_apart(pool, sem, value, passed):
    wait(pool, sem, value)
    pool.sem_inc(passed, 1)


class At:

    def __init__(self, b, u, total):
        self.b, self.u, self.total = b, u, total
        self.s = b * U + u + 1
        self.exists = not isinstance(self.s, int) or 1 <= self.s <= total

    def back(self, k):
        if isinstance(self.b, int):
            s = self.s - k - 1
            return At(s // U, s % U, self.total)
        carry = (self.u - k) // U
        return At(self.b + carry, (self.u - k) % U, self.total)

    def uses(self, ring, each):
        return (self.s - 1 - self.u % ring) * (each // ring)


def steps(eng, total, extra, body):
    for s in range(2 * U):
        body(At(s // U, s % U, total))
    with eng.Fori(2, total // U - 1, 1) as b:
        for u in range(U):
            body(At(b, u, total))
    for s in range(total - U, total + extra):
        body(At(s // U, s % U, total))


def layer_kernel(nc, x, ctx, Wk, bk, Wq, bq, Wv, bv, Wck, bck, Wcq, bcq, Wcv, bcv, Wp, bp,
                 gate_w, gate_b, w1, b1, w2, b2, out):
    def dram(name, shape, dt):
        return nc.dram_tensor(name, shape, dt).ap()

    q_d = dram("q_parts", [B, PARTS * D, 2, H * S], BF16)
    k_d = dram("k_parts", [B, PARTS * D, 1, H * S], BF16)
    ck_d = dram("ck_parts", [PARTS * D, H, B * SC], BF16)
    v_d = dram("v_rows", [B, S, H * HD], F32)
    cv_d = dram("cv_rows", [B * SC, H * HD], F32)
    y_d = dram("attention", [B, U, S, G * D], F32)
    xn_d = dram("xn_rows", [N + P, C], F32)
    tab_d = dram("slot_table", [CAP * E, 2], I32)
    bias_d = dram("bias_parts", [PARTS, ROWS, C], BF16)

    with ExitStack() as whole:
        ps = whole.enter_context(nc.psum_tensor("ps", [P, 8, 512], F32))
        ident = whole.enter_context(nc.sbuf_tensor("ident", [P, P], F32))
        identb = whole.enter_context(nc.sbuf_tensor("identb", [P, P], BF16))
        w1_sb = whole.enter_context(nc.sbuf_tensor("w1_sb", [P, U, KC, F], F32))
        w2_sb = whole.enter_context(nc.sbuf_tensor("w2_sb", [P, U, FC, C], F32))
        ks = whole.enter_context(nc.sbuf_tensor("ks", [P, U, 1, G, S], BF16))
        cks = whole.enter_context(nc.sbuf_tensor("cks", [P, U, G, SC], BF16))
        cvs = whole.enter_context(nc.sbuf_tensor("cvs", [P, U, 2, 2 * HD], F32))
        maskb = whole.enter_context(nc.sbuf_tensor("maskb", [P, P], BF16))
        wp_sb = whole.enter_context(nc.sbuf_tensor("wp_sb", [P, KC, C], F32))
        gw_sb = whole.enter_context(nc.sbuf_tensor("gw_sb", [P, KC, E], F32))
        bp_sb = whole.enter_context(nc.sbuf_tensor("bp_sb", [PARTS, C], BF16))
        gb_sb = whole.enter_context(nc.sbuf_tensor("gb_sb", [PARTS, E], BF16))
        route_in = whole.enter_context(nc.semaphore("route_in"))
        route_weights = [(wp_sb, Wp.rearrange("(c p) n -> p c n", p=P)), (gw_sb, gate_w.rearrange("(c p) n -> p c n", p=P)),
                         (bp_sb, bias_d[:, BP]), (gb_sb, bias_d[:, GB, 0:E])]
        w_in = [whole.enter_context(nc.semaphore(f"w_in{r}")) for r in range(U)]

        project(nc, ps, ident, identb, x, ctx, Wk, bk, Wq, bq, Wv, bv, Wck, bck, Wcq, bcq, Wcv, bcv, bp, gate_b, b2, bias_d,
                q_d, k_d, ck_d, v_d, cv_d, xn_d, tab_d, out, ks, cks, cvs, maskb)
        attend(nc, ps, ident, identb, ks, cks, cvs, maskb, q_d, k_d, ck_d, v_d, cv_d, y_d, w1, w2, w1_sb, w2_sb, w_in,
               route_weights, route_in)
        route(nc, ps, ident, x, wp_sb, gw_sb, bp_sb, gb_sb, route_in, y_d, xn_d, tab_d, out)
        experts(nc, ps, ident, w1, b1, w2, xn_d, tab_d, bias_d, out, w1_sb, w2_sb, w_in)


def load_expert(eng, w1, w2, w1_sb, w2_sb, w_in, e, ring):
    eng.dma_start(w1_sb[:, ring], w1[bass.ds(e, 1)].rearrange("e (c p) f -> p (e c) f", p=P)).then_inc(w_in[ring], 16)
    eng.dma_start(w2_sb[:, ring], w2[bass.ds(e, 1)].rearrange("e (c p) d -> p (e c) d", p=P)).then_inc(w_in[ring], 16)


def project(nc, ps, ident, identb, x, ctx, Wk, bk, Wq, bq, Wv, bv, Wck, bck, Wcq, bcq, Wcv, bcv, bp, gate_b, b2, bias_d,
            q_d, k_d, ck_d, v_d, cv_d, xn_d, tab_d, out, ks, cks, cvs, maskb):
    NCH = 3 * KC
    RING = NCH
    with ExitStack() as st:
        def sb(name, shape, dt):
            return st.enter_context(nc.sbuf_tensor(name, shape, dt))

        def sem(name):
            return st.enter_context(nc.semaphore("p_" + name))

        wq_sb, wk_sb, wcq_sb, wv_sb = (sb(n, [P, KC, C], F32) for n in ("wq_sb", "wk_sb", "wcq_sb", "wv_sb"))
        wck_sb, wcv_sb = (sb(n, [P, C], F32) for n in ("wck_sb", "wcv_sb"))
        bias = sb("bias", [P, 4, KC], F32)
        scaled = sb("scaled", [P, 4, KC], F32)
        bv_sb, bcv_sb = (sb(n, [P, C], F32) for n in ("bv_sb", "bcv_sb"))
        x_sb = sb("x_sb", [P, 2, NT, C], F32)
        xn_sb = sb("xn_sb", [P, 2, NT, C], F32)
        xT = sb("xT", [P, 2, KC, S], F32)
        cx = sb("cx", [P, NT, CC], F32)
        cxT = sb("cxT", [P, S], F32)
        stats = sb("stats", [P, NT, 6], F32)
        mv = sb("mv", [P, NT, 2], F32)
        base = sb("base", [P, NT], F32)
        rstd = sb("rstd", [P, NT], F32)
        power = sb("power", [P, NT], F32)
        full = sb("full", [P, RING, S], F32)
        rest = sb("rest", [P, RING, S], F32)
        parts = sb("parts", [P, RING, PARTS, S], BF16)
        va = sb("va", [P, NT, H, HD], F32)
        zero = sb("zero", [P, C], F32)
        ids = sb("ids", [P, E, 2], I32)
        biases, biases_rest = sb("biases", [ROWS, C], F32), sb("biases_rest", [ROWS, C], F32)
        biases_parts = sb("biases_bf", [ROWS, PARTS, C], BF16)

        consts, w_ready, c_in = sem("consts"), sem("w_ready"), sem("c_in")
        x_in = [sem("x_in0"), sem("x_in1")]
        bias_ready, var_ready, rstd_ready, xn_ready = (sem(n) for n in ("bias", "var", "rstd", "xn"))
        cT_psum, cT_ready, xT_psum, xT_ready = (sem(n) for n in ("cT_psum", "cT_ready", "xT_psum", "xT_ready"))
        chunk_psum, full_ready, rest_ready, second_ready, parts_ready = (
            sem(n) for n in ("chunk_psum", "full", "rest", "second", "parts"))
        parts_out = [sem(f"parts_out{r}") for r in range(RING)]
        v_psum, v_ready, v_out = sem("v_psum"), sem("v_ready"), sem("v_out")
        init_out, passed = sem("init_out"), sem("passed")
        biases_zero, biases_in, biases_ready = (sem(n) for n in ("biases_zero", "biases_in", "biases_ready"))
        weights = [(wq_sb, 0, q_d, 0), (wk_sb, 1, k_d, 0), (wcq_sb, 2, q_d, 1)]
        LOADS = 12
        blk = st.enter_context(nc.Block())

        def chunk(b, n):
            return KC + NCH * b + n

        def ring(n):
            return chunk(0, n) % RING

        def tile(b, t):
            return NT + NT * b + t

        def batches(eng, body):
            for u in range(2):
                body(u, u, False)
            with eng.Fori(1, B // 2 - 1, 1) as i:
                for u in range(2):
                    body(i * 2 + u, u, False)
            for u in range(2):
                body(B - 2 + u, u, u == 1)

        @blk.sync
        def _(sp):
            def load_x(b, u):
                wait(sp, xn_ready, b - 1)
                sp.dma_start(x_sb[:, u], x[bass.ds(b, 1)].rearrange("b (t p) c -> p (b t) c", p=P)).then_inc(x_in[u], 16)

            def store_parts(g, par, dst):
                sp.wait_ge(parts_ready, g + 1)
                for i in range(PARTS):
                    sp.dma_start(dst(i), parts[:, par, i, :]).then_inc(parts_out[par], 16)

            def store_values(g, dst):
                sp.wait_ge(v_ready, g + NT)
                sp.dma_start(dst.rearrange("(t p) f -> p t f", p=P), va[:].rearrange("p t h f -> p t (h f)")).then_inc(v_out, 16)

            load_x(0, 0)
            for w, d in ((Wck, wck_sb), (Wcv, wcv_sb)):
                sp.dma_start(d[:], w).then_inc(w_ready, 16)
            for w, d in ((Wq, wq_sb), (Wk, wk_sb), (Wcq, wcq_sb), (Wv, wv_sb)):
                sp.dma_start(d[:], w.rearrange("(c p) n -> p c n", p=P)).then_inc(w_ready, 16)
            with nc.allow_non_contiguous_dma(reason="biases by channel"):
                for i, b_ in enumerate((bq, bk, bcq, bck)):
                    sp.dma_start(bias[:, i, :], b_.rearrange("(c p) -> p c", p=P)).then_inc(w_ready, 16)
            for b_, d in ((bv, bv_sb), (bcv, bcv_sb)):
                sp.dma_start(d[:], b_.rearrange("(a c) -> a c", a=1).to_broadcast([P, C])).then_inc(w_ready, 16)
            load_x(1, 1)
            for g in range(KC):
                store_parts(g, g, lambda i: ck_d[i * D:(i + 1) * D, g * (H // KC):(g + 1) * (H // KC), :].rearrange("d h n -> h d n"))
            store_values(0, cv_d)

            def batch(b, u, last):
                for n in range(NCH):
                    (dst, which), oc = weights[n // KC][2:], n % KC
                    rows = dst[bass.ds(b, 1), :, which, oc * (H // KC) * S:(oc + 1) * (H // KC) * S]
                    store_parts(chunk(b, n), ring(n), lambda i: rows[:, i * D:(i + 1) * D].rearrange("b d (h n) -> (b h) d n", n=S))
                    if n == 3 and not (last or (isinstance(b, int) and b >= B - 2)):
                        load_x(b + 2, u)
                store_values(tile(b, 0), v_d[bass.ds(b, 1)].rearrange("b n f -> (b n) f"))

            batches(sp, batch)
            for par in range(RING):
                sp.wait_ge(parts_out[par], 16 * PARTS * len(range(par, chunk(B, 0), RING)))
            sp.wait_ge(v_out, 16 * (B + 1))

        @blk.gpsimd
        def _(pool):
            def deviations(b):
                pool.wait_ge(var_ready, b + 1)
                pool.tensor_tensor(rstd[:], base[:], power[:], ALU.pow).then_inc(rstd_ready, 1)

            pool.memset(ident[:], 0.0)
            pool.memset(power[:], -0.5)
            pool.memset(zero[:], 0.0)
            pool.memset(va[:], 1.0)
            pool.memset(ids[:], 0)
            pool.drain()
            pool.affine_select(out=ident[:], in_=ident[:], compare_op=ALU.not_equal, fill=1.0, base=0,
                               pattern=[[-1, P]], channel_multiplier=1)
            pool.iota(ids[:, :, 0], pattern=[[0, E]], base=N, channel_multiplier=1)
            pool.drain()
            pool.tensor_copy(identb[:], ident[:]).then_inc(consts, 1)
            deviations(0)
            pool.wait_ge(consts, 1)
            pool.dma_start(xn_d[N:N + P, :], zero[:]).then_inc(init_out, 16)
            pool.dma_start(out[N:N + P, :], zero[:]).then_inc(init_out, 16)
            pool.dma_start(tab_d.rearrange("(p e) t -> p (e t)", p=P), ids[:].rearrange("p e t -> p (e t)")).then_inc(init_out, 16)
            pool.wait_ge(biases_in, 48)
            pool.tensor_copy(biases_parts[:, 0], biases[:])
            pool.drain()
            pool.tensor_tensor(biases_rest[:], biases[:], biases_parts[:, 0], ALU.subtract)
            pool.drain()
            pool.tensor_copy(biases_parts[:, 1], biases_rest[:])
            pool.drain()
            pool.tensor_tensor(biases_parts[:, 2], biases_rest[:], biases_parts[:, 1], ALU.subtract).then_inc(biases_ready, 1)
            pool.wait_ge(biases_ready, 1)
            pool.dma_start(bias_d.rearrange("i e c -> e i c"), biases_parts[:]).then_inc(init_out, 16)
            pool.drain()
            pool.memset(maskb[:], 0.0)
            pool.drain()
            pool.memset(cvs[:], 0.0)
            pool.drain()
            pool.memset(ks[KQ:P], 1.0)
            pool.drain()
            pool.memset(cks[KQ:P], 1.0)
            pool.drain()
            pool.affine_select(out=maskb[:], in_=maskb[:], compare_op=ALU.is_ge, fill=LOW, base=0,
                               pattern=[[-1, P]], channel_multiplier=1)
            with pool.Fori(1, B, 1) as b:
                deviations(b)
            pool.wait_ge(init_out, 64)

        @blk.tensor
        def _(pe):
            def transposes(b, u):
                pe.wait_ge(xn_ready, b + 1)
                wait(pe, xT_ready, b)
                for c in range(KC):
                    for t in range(NT):
                        mm = pe.transpose(ps[:, c, t * P:(t + 1) * P], xn_sb[:, u, t, c * P:(c + 1) * P], ident[:])
                mm.then_inc(xT_psum, 1)

            pe.wait_ge(consts, 1)
            pe.wait_ge(c_in, 16)
            for t in range(NT):
                mm = pe.transpose(ps[:, 6, t * P:(t + 1) * P], cx[:, t, :], ident[:])
            mm.then_inc(cT_psum, 1)
            transposes(0, 0)
            pe.wait_ge(cT_ready, 1)
            pe.wait_ge(w_ready, 16 * LOADS)
            for oc in range(KC):
                pe.matmul(ps[:, 2 + oc, :], wck_sb[:, oc * P:(oc + 1) * P], cxT[:], start=True, stop=True).then_inc(chunk_psum, 1)
            for t in range(NT):
                wait(pe, v_ready, t - 1)
                pe.matmul(ps[:, 6 + t % 2, 0:C], cxT[:, t * P:(t + 1) * P], wcv_sb[:], start=True, stop=True).then_inc(v_psum, 1)

            def batch(b, u, last):
                pe.wait_ge(xT_ready, b + 1)
                for n in range(NCH):
                    w, oc = weights[n // KC][0], n % KC
                    g = chunk(b, n)
                    bank = 2 + chunk(u, n) % U
                    wait(pe, full_ready, g - 3)
                    for c in range(KC):
                        mm = pe.matmul(ps[:, bank, :], w[:, c, oc * P:(oc + 1) * P], xT[:, u, c, :],
                                       start=(c == 0), stop=(c == KC - 1))
                    mm.then_inc(chunk_psum, 1)
                if not last:
                    transposes(b + 1, 1 - u)
                for t in range(NT):
                    wait(pe, v_ready, tile(b, t) - 1)
                    for c in range(KC):
                        mm = pe.matmul(ps[:, 6 + t % 2, 0:C], xT[:, u, c, t * P:(t + 1) * P], wv_sb[:, c, :],
                                       start=(c == 0), stop=(c == KC - 1))
                    mm.then_inc(v_psum, 1)

            batches(pe, batch)

        @blk.scalar
        def _(act):
            def copy_x(b, u):
                act.wait_ge(xT_psum, b + 1)
                wait(act, v_psum, tile(b, 0) - NT)
                act.copy(xT[:, u, 0, :], ps[:, 0, :])
                act.copy(xT[:, u, 1, :], ps[:, 1, :]).then_inc(xT_ready, 1)

            def copy_chunk(g, par, bank, kind, oc):
                act.wait_ge(chunk_psum, g + 1)
                wait(act, parts_ready, g - RING + 1)
                wait(act, parts_out[par], 16 * PARTS // RING * (g - par))
                scale = SCALE if kind in (0, 2) else 1.0
                act.activation(parts[:, par, 0], ps[:, bank, :], ACT.Identity, bias=scaled[:, kind, oc:oc + 1], scale=scale)
                act.activation(full[:, par], ps[:, bank, :], ACT.Identity, bias=scaled[:, kind, oc:oc + 1],
                               scale=scale).then_inc(full_ready, 1)

            def second_part(g, par):
                act.wait_ge(rest_ready, g + 1)
                act.copy(parts[:, par, 1], rest[:, par]).then_inc(second_ready, 1)

            act.dma_start(cx[:], ctx.rearrange("b k c -> (b k) c").rearrange("(t p) c -> p t c", p=P)).then_inc(c_in, 16)
            act.dma_start(biases[0:E], b2).then_inc(biases_in, 16)
            act.wait_ge(biases_zero, 1)
            act.dma_start(biases[BP:BP + 1], bp.rearrange("(a c) -> a c", a=1)).then_inc(biases_in, 16)
            act.dma_start(biases[GB:GB + 1, 0:E], gate_b.rearrange("(a c) -> a c", a=1)).then_inc(biases_in, 16)
            act.wait_ge(cT_psum, 1)
            act.copy(cxT[:], ps[:, 6, :]).then_inc(cT_ready, 1)
            copy_x(0, 0)
            act.wait_ge(bias_ready, 1)
            for g in range(KC):
                copy_chunk(g, g, 2 + g, 3, g)
            for g in range(KC):
                second_part(g, g)

            def batch(b, u, last):
                for n in range(NCH):
                    copy_chunk(chunk(b, n), ring(n), 2 + chunk(u, n) % U, weights[n // KC][1], n % KC)
                    if n > 0:
                        second_part(chunk(b, n - 1), ring(n - 1))
                second_part(chunk(b, NCH - 1), ring(NCH - 1))
                if not last:
                    copy_x(b + 1, 1 - u)

            batches(act, batch)

        @blk.vector
        def _(dve):
            def variances(b, u):
                dve.wait_ge(x_in[u], 8 * (b - u) + 16)
                for t in range(NT):
                    dve.bn_stats(stats[:, t], x_sb[:, u, t])
                dve.drain()
                for t in range(NT):
                    dve.bn_aggr(mv[:, t], stats[:, t])
                dve.drain()
                dve.tensor_scalar(base[:], mv[:, :, 1], EPS, None, ALU.add).then_inc(var_ready, 1)

            def normalise(b, u):
                dve.wait_ge(rstd_ready, b + 1)
                wait(dve, xT_psum, b - 1)
                for t in range(NT):
                    last = dve.tensor_scalar(xn_sb[:, u, t], x_sb[:, u, t], mv[:, t, 0:1], rstd[:, t:t + 1],
                                             ALU.subtract, ALU.mult)
                last.then_inc(xn_ready, 1)
                dve.drain()

            def subtract_first(g, par):
                dve.wait_ge(full_ready, g + 1)
                dve.tensor_tensor(rest[:, par], full[:, par], parts[:, par, 0], ALU.subtract).then_inc(rest_ready, 1)

            def third_part(g, par):
                dve.wait_ge(second_ready, g + 1)
                dve.tensor_tensor(parts[:, par, 2], rest[:, par], parts[:, par, 1], ALU.subtract).then_inc(parts_ready, 1)

            def values(done, t, b_sb):
                dve.wait_ge(v_psum, done * NT + t + 1)
                if t == 0:
                    wait(dve, v_out, 16 * done)
                dve.tensor_tensor(va[:, t, :, 0:D], ps[:, 6 + t % 2, 0:C].rearrange("p (h d) -> p h d", d=D),
                                  b_sb[:].rearrange("p (h d) -> p h d", d=D), ALU.add).then_inc(v_ready, 1)

            dve.memset(biases[E:ROWS], 0.0).then_inc(biases_zero, 1)
            variances(0, 0)
            normalise(0, 0)
            dve.wait_ge(w_ready, 16 * LOADS)
            dve.tensor_copy(scaled[:], bias[:])
            dve.drain()
            dve.tensor_scalar(scaled[:, 0], bias[:, 0], SCALE, None, ALU.mult)
            dve.tensor_scalar(scaled[:, 2], bias[:, 2], SCALE, None, ALU.mult).then_inc(bias_ready, 1)
            dve.wait_ge(consts, 1)
            for g in range(KC):
                subtract_first(g, g)
            for g in range(KC):
                third_part(g, g)
            for t in range(NT):
                values(0, t, bcv_sb)

            def batch(b, u, last):
                for n in range(NCH):
                    subtract_first(chunk(b, n), ring(n))
                    if n > 0:
                        third_part(chunk(b, n - 1), ring(n - 1))
                    if n == 0 and not last:
                        variances(b + 1, 1 - u)
                    if n == 2 and not last:
                        normalise(b + 1, 1 - u)
                for t in range(NT):
                    values(b + 1, t, bv_sb)
                    if t == 1:
                        third_part(chunk(b, NCH - 1), ring(NCH - 1))

            batches(dve, batch)


def attend(nc, ps, ident, identb, ks, cks, cvs, maskb, q_d, k_d, ck_d, v_d, cv_d, y_d, w1, w2, w1_sb, w2_sb, w_in,
           route_weights, route_in):
    TOTAL = B * U
    QK_LOADS = 6
    with ExitStack() as st:
        def sb(name, shape, dt):
            return st.enter_context(nc.sbuf_tensor(name, shape, dt))

        def sem(name):
            return st.enter_context(nc.semaphore("a_" + name))

        qs = sb("qs", [P, U, 2, G, S], BF16)
        ck_all = sb("ck_all", [P, H, B * SC], BF16)
        vs = sb("vs", [P, U, NT, G * HD], F32)
        negm = sb("negm", [P, 2, 2 * G * NT], F32)
        mrest = sb("mrest", [P, 2 * G * NT], F32)
        mparts = sb("mparts", [P, PARTS, 2 * G * NT], BF16)
        mT = sb("mT", [PARTS * 2 * G * NT, P], BF16)
        pt = sb("pt", [P, 2, G, PW], F32)
        ptc = sb("ptc", [P, 2, 2, S], F32)
        o_sb = sb("o_sb", [P, 2, S], F32)
        recip = sb("recip", [P, 2, NT * G], F32)
        y2 = sb("y2", [P, 2, NT * G, D], F32)
        y_sb = sb("y_sb", [P, 2, NT, G * D], F32)

        passed = sem("passed")
        qk_in = [sem(f"qk_in{r}") for r in range(U)]
        v_in = [sem(f"v_in{r}") for r in range(U)]
        m_in = [sem("m_in0"), sem("m_in1")]
        y_out = [sem("y_out0"), sem("y_out1")]
        a_psum, a_max, m_split, mT_psum, mT_ready = (sem(n) for n in ("a_psum", "a_max", "m_split", "mT_psum", "mT_ready"))
        ck_in, ck_ready = sem("ck_in"), sem("ck_ready")
        b_psum, b_exp, masked = (sem(n) for n in ("b_psum", "b_exp", "masked"))
        o_psum, o_copied, oT_psum, oT_read, y_ready = (
            sem(n) for n in ("o_psum", "o_copied", "oT_psum", "oT_read", "y_ready"))
        blk = st.enter_context(nc.Block())

        @blk.sync
        def _(sp):
            def load_qk(a):
                wait(sp, b_psum, NB * (a.s - U))
                heads = slice(a.u * G * S, (a.u + 1) * G * S)
                row = 0
                for n in (3, 2, 1):
                    rows = slice(row, row + n * D)
                    sp.dma_start(qs[rows, a.u].rearrange("p s h n -> p s (h n)"),
                                 q_d[bass.ds(a.b, 1), 0:n * D, :, heads].rearrange("b r s n -> (b r) s n")).then_inc(qk_in[a.u], 16)
                    part = 3 - n
                    sp.dma_start(ks[rows, a.u, 0].rearrange("p h n -> p (h n)"),
                                 k_d[bass.ds(a.b, 1), part * D:(part + 1) * D, 0, heads].to_broadcast([n, D, G * S])
                                 ).then_inc(qk_in[a.u], 16)
                    row += n * D

            def load_v(a):
                wait(sp, o_psum, a.s - U)
                sp.dma_start(vs[:, a.u], v_d[bass.ds(a.b, 1), :, a.u * G * HD:(a.u + 1) * G * HD].rearrange("b (t p) f -> p (b t) f", p=P)).then_inc(v_in[a.u], 16)
                for half in range(2):
                    src = cv_d[bass.ds(a.b * SC, SC), a.u * G * HD:(a.u + 1) * G * HD].rearrange("k (r f) -> k r f", f=2 * HD)
                    sp.dma_start(cvs[half * SC:(half + 1) * SC, a.u, :, half * HD:(half + 1) * HD],
                                 src[:, :, half * HD:(half + 1) * HD]).then_inc(v_in[a.u], 16)

            def load_m(a):
                sp.wait_ge(mT_ready, a.s)
                sp.dma_start(qs[KQ:KM, a.u].rearrange("p s h n -> p (s h n)"), mT[:]).then_inc(m_in[a.u % 2], 16)

            def store_y(a):
                sp.wait_ge(y_ready, a.s)
                sp.dma_start(y_d[bass.ds(a.b, 1), a.u].rearrange("b (t p) f -> p (b t) f", p=P), y_sb[:, a.u % 2]
                             ).then_inc(y_out[a.u % 2], 16)

            def step(a):
                if a.back(-1).exists:
                    load_qk(a.back(-1))
                if a.back(1).exists:
                    load_m(a.back(1))
                if a.exists:
                    load_v(a)
                if a.back(3).exists:
                    store_y(a.back(3))
                if isinstance(a.s, int) and a.s == TOTAL + 2:
                    for dst, src in route_weights:
                        sp.dma_start(dst[:], src).then_inc(route_in, 16)
                if isinstance(a.s, int) and a.s > TOTAL - U and a.exists:
                    load_expert(sp, w1, w2, w1_sb, w2_sb, w_in, a.u, a.u)

            load_qk(At(0, 0, TOTAL))
            for i, part in enumerate(KPARTS):
                sp.dma_start(ck_all[i * D:(i + 1) * D].rearrange("p h n -> p (h n)"),
                             ck_d[part * D:(part + 1) * D].rearrange("d h n -> d (h n)")).then_inc(ck_in, 16)
            steps(sp, TOTAL, 3, step)
            for par in range(2):
                sp.wait_ge(y_out[par], 8 * TOTAL)

        @blk.gpsimd
        def _(pool):
            def copy_ck(a):
                wait(pool, b_psum, NB * (a.s - U))
                pool.tensor_copy(cks[0:KQ, a.u], ck_all[0:KQ, a.u * G:(a.u + 1) * G, bass.ds(a.b * SC, SC)]).then_inc(ck_ready, 1)

            pool.wait_ge(ck_in, 16 * len(KPARTS))
            copy_ck(At(0, 0, TOTAL))

            def split_maxima(a):
                m = negm[:, a.u % 2]
                wait_apart(pool, a_max, NA * a.s, passed)
                wait_apart(pool, mT_psum, a.s - 1, passed)
                pool.tensor_copy(mparts[:, 0], m)
                pool.drain()
                pool.tensor_tensor(mrest[:], m, mparts[:, 0], ALU.subtract)
                pool.drain()
                pool.tensor_copy(mparts[:, 1], mrest[:])
                pool.drain()
                pool.tensor_tensor(mparts[:, 2], mrest[:], mparts[:, 1], ALU.subtract).then_inc(m_split, 1)

            def add_outputs(a):
                pool.wait_ge(oT_read, a.s)
                wait(pool, y_out[a.u % 2], a.uses(2, 16))
                pool.tensor_tensor(y_sb[:, a.u % 2].rearrange("p t f -> p (t f)"), y2[:, 0].rearrange("p x d -> p (x d)"),
                                   y2[:, 1].rearrange("p x d -> p (x d)"), ALU.add).then_inc(y_ready, 1)

            def step(a):
                if a.back(1).exists:
                    split_maxima(a.back(1))
                if a.back(-1).exists:
                    copy_ck(a.back(-1))
                x = a.back(2)
                if x.exists:
                    wait_apart(pool, b_exp, NB * (x.s - 1) + NB - 1, passed)
                    for j in range(NT):
                        block = pt[:, x.u % 2, :, OFF[j]:OFF[j] + P]
                        pool.affine_select(out=block, in_=block, compare_op=ALU.is_ge, fill=0.0, base=0,
                                           pattern=[[0, G], [1, P]], channel_multiplier=-1).then_inc(masked, 1)
                if a.back(3).exists:
                    add_outputs(a.back(3))

            steps(pool, TOTAL, 3, step)

        @blk.tensor
        def _(pe):
            def scores_by_query(a, k):
                g = NA * (a.s - 1) + k
                bank = (NA * a.u + k) % 2
                wait(pe, a_max, g - 1)
                if k < 11:
                    t = 0 if k < 1 else 1 if k < 3 else 2 if k < 7 else 3
                    first, count = ((0, 4), (0, 2), (2, 2), *((h, 1) for h in range(4)), *((h, 1) for h in range(4)))[k]
                    w = P * (t + 1)
                    for i in range(count):
                        h = first + i
                        pe.matmul(ps[:, bank, i * w:(i + 1) * w], qs[0:KQ, a.u, 0, h, t * P:(t + 1) * P], ks[0:KQ, a.u, 0, h, 0:w],
                                  start=True, stop=False)
                        mm = pe.matmul(ps[:, bank, i * w + t * P:(i + 1) * w], identb[:], maskb[:], start=False, stop=True)
                else:
                    if k == 11:
                        pe.wait_ge(ck_ready, a.s)
                    for i in range(2):
                        t = 2 * (k - 11) + i
                        for h in range(G):
                            at = (i * G + h) * SC
                            mm = pe.matmul(ps[:, bank, at:at + SC], qs[0:KQ, a.u, 1, h, t * P:(t + 1) * P], cks[0:KQ, a.u, h, :],
                                           start=True, stop=True)
                mm.then_inc(a_psum, 1)

            def maxima_to_rows(a):
                pe.wait_ge(m_split, a.s)
                wait(pe, oT_read, a.s - 3)
                pe.transpose(ps[0:mT.shape[0], 7, 0:P // 2].bitcast(BF16), mparts[:].rearrange("p i m -> p (i m)"), identb[:]
                             ).then_inc(mT_psum, 1)

            def scores_by_key(a, k):
                g = NB * (a.s - 1) + k
                bank = 2 + 2 * ((NB * a.u + k) % 2)
                wait(pe, b_exp, g - 1)
                if k == 0:
                    pe.wait_ge(m_in[a.u % 2], a.uses(2, 16) + 16)
                if k == 6:
                    for h in range(G):
                        r = (h % 2) * SC
                        mm = pe.matmul(ps[r:r + SC, bank + h // 2, :], cks[0:KM, a.u, h, :], qs[0:KM, a.u, 1, h, :],
                                       start=True, stop=True)
                else:
                    todo = [(2 * (k // 3) + k % 3, j, j, 0) for j in (0, 1)] if k % 3 < 2 else \
                        [(2 * (k // 3) + i, j, i, OFF[j] - OFF[2]) for i in (0, 1) for j in (2, 3)]
                    for h, j, bk_, at in todo:
                        mm = pe.matmul(ps[:, bank + bk_, at:at + WID[j]], ks[0:KM, a.u, 0, h, j * P:(j + 1) * P],
                                       qs[0:KM, a.u, 0, h, j * P:S], start=True, stop=True)
                mm.then_inc(b_psum, 1)

            def outputs(a, j):
                if j == 0:
                    wait(pe, oT_read, a.s - 1)
                    pe.wait_ge(masked, NT * a.s)
                    pe.wait_ge(v_in[a.u], a.uses(4, 48) + 48)
                for h in range(G):
                    pe.matmul(ps[h * HD:(h + 1) * HD, 6, j * P:S], vs[:, a.u, j, h * HD:(h + 1) * HD],
                              pt[:, a.u % 2, h, OFF[j]:OFF[j] + WID[j]], start=(j == 0), stop=(j == NT - 1))

            def cross_outputs(a):
                pe.wait_ge(b_exp, NB * a.s)
                if a.back(-2).exists:
                    pe.wait_ge(mT_ready, a.s + 2)
                for r in range(2):
                    mm = pe.matmul(ps[r * SC:(r + 1) * SC, 7, :], cvs[:, a.u, r, :], ptc[:, a.u % 2, r, :], start=True, stop=True)
                mm.then_inc(o_psum, 1)

            def outputs_by_token(a):
                pe.wait_ge(o_copied, a.s)
                for i in range(2):
                    for t in range(NT):
                        mm = pe.transpose(ps[:, 6 + i, t * P:(t + 1) * P], o_sb[:, i, t * P:(t + 1) * P], ident[:])
                mm.then_inc(oT_psum, 1)

            def step(a):
                m, b, o = a.back(1), a.back(2), a.back(3)

                def A(*ks_):
                    for k in ks_:
                        if a.exists:
                            if k == 0:
                                pe.wait_ge(qk_in[a.u], a.uses(4, 16 * QK_LOADS) + 16 * QK_LOADS)
                            scores_by_query(a, k)

                def BK(k):
                    if b.exists:
                        scores_by_key(b, k)

                def CO(j):
                    if o.exists:
                        outputs(o, j)

                A(0)
                BK(0)
                A(1)
                CO(0)
                A(2)
                BK(1)
                A(3)
                CO(1)
                A(4)
                if m.exists:
                    maxima_to_rows(m)
                BK(2)
                A(5)
                CO(2)
                A(6)
                BK(3)
                A(7)
                CO(3)
                if o.exists:
                    cross_outputs(o)
                A(8)
                BK(4)
                A(9)
                BK(5)
                A(10)
                if o.exists:
                    outputs_by_token(o)
                A(11)
                BK(6)
                A(12)

            steps(pe, TOTAL, 3, step)

        @blk.scalar
        def _(act):
            def exponentials(a, k):
                bank = 2 + 2 * ((NB * a.u + k) % 2)
                act.wait_ge(b_psum, NB * (a.s - 1) + k + 1)
                if k == 0:
                    wait(act, o_psum, a.s - 2)
                two = ps[:, bank:bank + 2, :]
                if k == 6:
                    src, dst = two, ptc[:, a.u % 2]
                elif k % 3 < 2:
                    w = WID[0] + WID[1]
                    src, dst = two.rearrange("p b n -> p (b n)")[:, 0:w], pt[:, a.u % 2, 2 * (k // 3) + k % 3, 0:w]
                else:
                    src, dst = two[:, :, 0:PW - OFF[2]], pt[:, a.u % 2, 2 * (k // 3):2 * (k // 3) + 2, OFF[2]:PW]
                act.activation(dst, src, ACT.Exp).then_inc(b_exp, 1)

            def step(a):
                b, o = a.back(2), a.back(3)
                for k in range(NB):
                    if b.exists:
                        exponentials(b, k)
                    if k == 3 and o.exists:
                        act.wait_ge(o_psum, o.s)
                        wait(act, oT_psum, o.s - 1)
                        act.copy(o_sb[:, 0], ps[:, 6, :])
                        act.copy(o_sb[:, 1], ps[:, 7, :]).then_inc(o_copied, 1)

            steps(act, TOTAL, 3, step)

        @blk.vector
        def _(dve):
            def maxima(a, k):
                bank, m = (NA * a.u + k) % 2, negm[:, a.u % 2]
                dve.wait_ge(a_psum, NA * (a.s - 1) + k + 1)
                if k == 0:
                    wait(dve, m_split, a.s - 2)
                if k == 0:
                    dst, src = m[:, 0:G * NT:NT], ps[:, bank, :].rearrange("p (h n) -> p h n", h=G)
                elif k < 3:
                    lo = 2 * (k - 1) * NT + 1
                    dst, src = m[:, lo:lo + NT + 1:NT], ps[:, bank, :].rearrange("p (h n) -> p h n", h=2)
                elif k < 11:
                    h, t = (k - 3) % 4, 2 + (k - 3) // 4
                    dst, src = m[:, h * NT + t:h * NT + t + 1], ps[:, bank, 0:(t + 1) * P]
                else:
                    t = 2 * (k - 11)
                    dst = m[:, G * NT:].rearrange("p (h t) -> p t h", t=NT)[:, t:t + 2, :]
                    src = ps[:, bank, :].rearrange("p (t h n) -> p t h n", t=2, h=G)
                dve.tensor_reduce(dst, src, AX.X, ALU.max, negate=True).then_inc(a_max, 1)

            def copy_maxima(a):
                dve.wait_ge(mT_psum, a.s)
                if a.back(1).exists:
                    x = a.back(1)
                    wait(dve, m_in[x.u % 2], x.uses(2, 16) + 16)
                dve.tensor_copy(mT[:], ps[0:mT.shape[0], 7, 0:P // 2].bitcast(BF16)).then_inc(mT_ready, 1)

            def normalise(a):
                dve.wait_ge(oT_psum, a.s)
                for i in range(2):
                    heads = ps[:, 6 + i, :].rearrange("p (x f) -> p x f", f=HD)
                    dve.reciprocal(recip[:, i].rearrange("p (x o) -> p x o", o=1), heads[:, :, D:D + 1])
                dve.drain()
                wait(dve, y_ready, a.s - 1)
                for i in range(2):
                    heads = ps[:, 6 + i, :].rearrange("p (x f) -> p x f", f=HD)
                    last = dve.tensor_tensor(y2[:, i], heads[:, :, 0:D],
                                             recip[:, i].rearrange("p (x o) -> p x o", o=1).to_broadcast([P, NT * G, D]), ALU.mult)
                last.then_inc(oT_read, 1)

            def step(a):
                m, o = a.back(1), a.back(3)
                for k in range(NA):
                    if a.exists:
                        maxima(a, k)
                    if k == 4 and m.exists:
                        copy_maxima(m)
                    if k == 10 and o.exists:
                        normalise(o)
            steps(dve, TOTAL, 3, step)


def route(nc, ps, ident, x, wp_sb, gw_sb, bp_sb, gb_sb, route_in, y_d, xn_d, tab_d, out):
    TOTAL = N // P
    with ExitStack() as st:
        def sb(name, shape, dt):
            return st.enter_context(nc.sbuf_tensor(name, shape, dt))

        def sem(name):
            return st.enter_context(nc.semaphore("r_" + name))

        one = sb("one", [PARTS, P], BF16)
        before = sb("before", [P, P], BF16)
        ones = sb("ones", [P, P], BF16)
        expert = sb("expert", [P, E], F32)
        token = sb("token", [P, 1], F32)
        y_in = sb("y_in_sb", [P, U, U, G * D], F32)
        x_in_sb = sb("x_in_sb", [P, U, C], F32)
        yT = sb("yT", [P, U, KC, P], F32)
        x1 = sb("x1", [P, U, C], F32)
        stats, mv = sb("r_stats", [P, 6], F32), sb("r_mv", [P, U, 2], F32)
        base, rstd, power = sb("r_base", [P, U], F32), sb("r_rstd", [P, U], F32), sb("r_power", [P, 1], F32)
        shift = sb("shift", [P, U], F32)
        xn = sb("xn", [P, U, C], F32)
        xnT = sb("xnT", [P, U, KC, P], F32)
        top = sb("top", [P, U, 8], F32)
        top_i = sb("top_i", [P, U, 8], U32)
        neg_top = sb("neg_top", [P, U], F32)
        hot = sb("hot", [P, U, TOPK, E], F32)
        chosen = sb("chosen", [P, U, E], BF16)
        sofar = sb("sofar", [P, U, E], BF16)
        picked = sb("picked", [P, TOPK, E], F32)
        place = sb("place", [P, TOPK], F32)
        slot = sb("slot", [P, U, TOPK], U32)
        eg = sb("eg", [P, U, TOPK], F32)
        esum = sb("esum", [P, U], F32)
        einv = sb("einv", [P, 1], F32)
        row = sb("row", [P, U, TOPK, 2], I32)

        consts, passed = sem("consts"), sem("passed")
        loaded = [sem(f"loaded{r}") for r in range(U)]
        x1_out = [sem(f"x1_out{r}") for r in range(U)]
        table_out = [sem(f"table_out{r}") for r in range(U)]
        yT_psum, yT_ready, p_psum, x1_ready = (sem(n) for n in ("yT_psum", "yT_ready", "p_psum", "x1"))
        var_ready, rstd_ready, shift_ready, xn_ready, xnT_psum, xnT_ready = (
            sem(n) for n in ("var", "rstd", "shift_ready", "xn", "xnT_psum", "xnT_ready"))
        lg_psum, top_ready, hot_ready, exp_ready, place_psum, row_ready = (
            sem(n) for n in ("lg_psum", "top", "hot", "exp", "place_psum", "row"))
        blk = st.enter_context(nc.Block())

        @blk.sync
        def _(sp):
            def load(a):
                wait(sp, yT_psum, a.s - U)
                wait(sp, x1_ready, a.s - U)
                sp.dma_start(y_in[:, a.u], y_d[bass.ds(a.b, 1), :, a.u * P:(a.u + 1) * P, :].rearrange("b g t f -> t (b g) f")
                             ).then_inc(loaded[a.u], 16)
                sp.dma_start(x_in_sb[:, a.u], x[bass.ds(a.b, 1), a.u * P:(a.u + 1) * P, :].rearrange("b t c -> (b t) c")
                             ).then_inc(loaded[a.u], 16)

            def store(a):
                sp.wait_ge(xn_ready, a.s)
                sp.dma_start(out[bass.ds(a.b * S + a.u * P, P), :], x1[:, a.u]).then_inc(x1_out[a.u], 16)
                sp.dma_start(xn_d[bass.ds(a.b * S + a.u * P, P), :], xn[:, a.u]).then_inc(x1_out[a.u], 16)

            def step(a):
                if a.back(-3).exists:
                    load(a.back(-3))
                if a.back(1).exists:
                    store(a.back(1))

            for u in range(3):
                load(At(0, u, TOTAL))
            steps(sp, TOTAL, 5, step)
            for r in range(U):
                sp.wait_ge(x1_out[r], 32 * (TOTAL // U))

        @blk.gpsimd
        def _(pool):
            pool.memset(before[:], 1.0)
            pool.memset(ones[:], 1.0)
            pool.memset(sofar[:], 0.0)
            pool.memset(one[:], 1.0)
            pool.memset(power[:], -0.5)
            pool.iota(expert[:], pattern=[[1, E]], base=0, channel_multiplier=0, allow_small_or_imprecise_dtypes=True)
            pool.iota(token[:], pattern=[[0, 1]], base=0, channel_multiplier=1, allow_small_or_imprecise_dtypes=True)
            pool.drain()
            pool.affine_select(out=before[:], in_=before[:], compare_op=ALU.is_gt, fill=0.0, base=0,
                               pattern=[[1, P]], channel_multiplier=-1).then_inc(consts, 1)

            def deviation(a):
                pool.wait_ge(var_ready, a.s)
                pool.tensor_tensor(rstd[:, a.u:a.u + 1], base[:, a.u:a.u + 1], power[:], ALU.pow).then_inc(rstd_ready, 1)

            def scatter(a):
                wait_apart(pool, row_ready, a.s, passed)
                for k in range(TOPK):
                    pool.indirect_dma_start(out=tab_d, out_offset=bass.IndirectOffsetOnAxis(ap=slot[:, a.u, k:k + 1], axis=0),
                                            in_=row[:, a.u, k, :], in_offset=None, bounds_check=CAP * E - 1,
                                            oob_is_err=False).then_inc(table_out[a.u], 16)

            def step(a):
                if a.back(1).exists:
                    deviation(a.back(1))
                if a.back(5).exists:
                    scatter(a.back(5))

            steps(pool, TOTAL, 5, step)
            for r in range(U):
                pool.wait_ge(table_out[r], 16 * TOPK * (TOTAL // U))

        @blk.tensor
        def _(pe):
            pe.wait_ge(route_in, 64)
            pe.wait_ge(consts, 1)

            def step(a):
                if a.exists:
                    pe.wait_ge(loaded[a.u], a.uses(4, 32) + 32)
                    wait(pe, yT_ready, a.s - 1)
                    for c in range(KC):
                        mm = pe.transpose(ps[:, 0, c * P:(c + 1) * P],
                                          y_in[:, a.u].rearrange("p g f -> p (g f)")[:, c * P:(c + 1) * P], ident[:])
                    mm.then_inc(yT_psum, 1)
                x_ = a.back(1)
                if x_.exists:
                    pe.wait_ge(yT_ready, x_.s)
                    wait(pe, x1_ready, x_.s - 2)
                    pe.matmul(ps[:, 1 + 4 * (x_.u % 2), 0:C], one[:], bp_sb[:], start=True, stop=False)
                    for c in range(KC):
                        mm = pe.matmul(ps[:, 1 + 4 * (x_.u % 2), 0:C], yT[:, x_.u, c, :], wp_sb[:, c, :], start=False, stop=(c == KC - 1))
                    mm.then_inc(p_psum, 1)
                x_ = a.back(2)
                if x_.exists:
                    pe.wait_ge(xn_ready, x_.s)
                    wait(pe, xnT_ready, x_.s - 1)
                    for c in range(KC):
                        mm = pe.transpose(ps[:, 2, c * P:(c + 1) * P], xn[:, x_.u, c * P:(c + 1) * P], ident[:])
                    mm.then_inc(xnT_psum, 1)
                x_ = a.back(3)
                if x_.exists:
                    pe.wait_ge(xnT_ready, x_.s)
                    wait(pe, top_ready, x_.s - 2)
                    pe.matmul(ps[:, 3 + 4 * (x_.u % 2), 0:E], one[:], gb_sb[:], start=True, stop=False)
                    for c in range(KC):
                        mm = pe.matmul(ps[:, 3 + 4 * (x_.u % 2), 0:E], xnT[:, x_.u, c, :], gw_sb[:, c, :], start=False, stop=(c == KC - 1))
                    mm.then_inc(lg_psum, 1)
                x_ = a.back(4)
                if x_.exists:
                    pe.wait_ge(hot_ready, x_.s)
                    wait(pe, row_ready, x_.s - 2)
                    pe.matmul(ps[:, 4 + 2 * (x_.u % 2), 0:E], before[:], chosen[:, x_.u, :], start=True, stop=False)
                    pe.matmul(ps[:, 4 + 2 * (x_.u % 2), 0:E], ones[:], sofar[:, x_.u, :], start=False, stop=True).then_inc(place_psum, 1)

            steps(pe, TOTAL, 5, step)

        @blk.scalar
        def _(act):
            def step(a):
                if a.exists:
                    act.wait_ge(yT_psum, a.s)
                    wait(act, p_psum, a.s - U)
                    act.copy(yT[:, a.u].rearrange("p c n -> p (c n)"), ps[:, 0, 0:C]).then_inc(yT_ready, 1)
                x_ = a.back(2)
                if x_.exists:
                    act.wait_ge(xnT_psum, x_.s)
                    wait(act, lg_psum, a.s - 5)
                    act.copy(xnT[:, x_.u].rearrange("p c n -> p (c n)"), ps[:, 2, 0:C]).then_inc(xnT_ready, 1)
                x_ = a.back(3)
                if x_.exists:
                    act.wait_ge(hot_ready, x_.s)
                    wait(act, row_ready, x_.s - U)
                    act.activation(eg[:, x_.u], top[:, x_.u, 0:TOPK], ACT.Exp, bias=neg_top[:, x_.u:x_.u + 1],
                                   accum_out=esum[:, x_.u:x_.u + 1]).then_inc(exp_ready, 1)
                x_ = a.back(1)
                if x_.exists:
                    act.wait_ge(shift_ready, x_.s)
                    wait(act, x1_out[x_.u], x_.uses(4, 32))
                    act.activation(xn[:, x_.u], x1[:, x_.u], ACT.Identity, bias=shift[:, x_.u:x_.u + 1],
                                   scale=rstd[:, x_.u:x_.u + 1]).then_inc(xn_ready, 1)

            steps(act, TOTAL, 5, step)

        @blk.vector
        def _(dve):
            dve.wait_ge(consts, 1)

            def step(a):
                r, c, f, e = (a.back(k) for k in (1, 3, 4, 5))
                if r.exists:
                    dve.wait_ge(p_psum, r.s)
                    dve.wait_ge(loaded[r.u], r.uses(4, 32) + 32)
                    wait(dve, x1_out[r.u], r.uses(4, 32))
                    dve.tensor_tensor(x1[:, r.u], ps[:, 1 + 4 * (r.u % 2), 0:C], x_in_sb[:, r.u], ALU.add).then_inc(x1_ready, 1)
                if e.exists:
                    dve.wait_ge(place_psum, e.s)
                    dve.wait_ge(exp_ready, e.s)
                    dve.tensor_tensor(picked[:], hot[:, e.u], ps[:, 4 + 2 * (e.u % 2), 0:E].rearrange("p (o e) -> p o e", o=1).to_broadcast([P, TOPK, E]),
                                      ALU.mult)
                    dve.reciprocal(einv[:], esum[:, e.u:e.u + 1])
                dve.drain()
                if r.exists:
                    dve.bn_stats(stats[:], x1[:, r.u])
                if f.exists:
                    dve.tensor_tensor(sofar[:, (f.u + 1) % U], sofar[:, f.u], chosen[:, f.u], ALU.add)
                if e.exists:
                    wait(dve, table_out[e.u], e.uses(4, 16 * TOPK))
                    dve.tensor_reduce(place[:], picked[:], AX.X, ALU.add)
                    dve.tensor_scalar(row[:, e.u, :, 1].bitcast(F32), eg[:, e.u], einv[:, 0:1], None, ALU.mult)
                    dve.tensor_copy(row[:, e.u, :, 0], token[:].to_broadcast([P, TOPK]))
                dve.drain()
                if r.exists:
                    dve.bn_aggr(mv[:, r.u], stats[:])
                if e.exists:
                    dve.tensor_scalar(token[:], token[:], float(P), None, ALU.add)
                    dve.scalar_tensor_tensor(out=slot[:, e.u], in0=place[:], scalar=float(E), in1=top_i[:, e.u, 0:TOPK],
                                             op0=ALU.mult, op1=ALU.add).then_inc(row_ready, 1)
                dve.drain()
                if c.exists:
                    dve.wait_ge(lg_psum, c.s)
                if r.exists:
                    dve.tensor_scalar(base[:, r.u:r.u + 1], mv[:, r.u, 1:2], EPS, None, ALU.add).then_inc(var_ready, 1)
                if c.exists:
                    logits = ps[:, 3 + 4 * (c.u % 2), 0:E]
                    dve.max(top[:, c.u], logits)
                    dve.drain()
                    dve.max_index(top_i[:, c.u], top[:, c.u], logits).then_inc(top_ready, 1)
                    dve.tensor_scalar(neg_top[:, c.u:c.u + 1], top[:, c.u, 0:1], -1.0, None, ALU.mult)
                    dve.drain()
                    dve.tensor_tensor(hot[:, c.u], expert[:].rearrange("p (o e) -> p o e", o=1).to_broadcast([P, TOPK, E]),
                                      top_i[:, c.u, 0:TOPK].rearrange("p (k o) -> p k o", o=1).to_broadcast([P, TOPK, E]), ALU.is_equal)
                if r.exists:
                    dve.wait_ge(rstd_ready, r.s)
                    dve.scalar_tensor_tensor(out=shift[:, r.u:r.u + 1], in0=mv[:, r.u, 0:1], scalar=-1.0, in1=rstd[:, r.u:r.u + 1],
                                             op0=ALU.mult, op1=ALU.mult).then_inc(shift_ready, 1)
                dve.drain()
                if c.exists:
                    wait(dve, place_psum, c.s - U + 1)
                    with nc.allow_low_precision(reason="counts up to three are exact"):
                        dve.tensor_reduce(chosen[:, c.u], hot[:, c.u].rearrange("p k e -> p e k"), AX.X, ALU.add).then_inc(hot_ready, 1)

            steps(dve, TOTAL, 5, step)


def experts(nc, ps, ident, w1, b1, w2, xn_d, tab_d, bias_d, out, w1_sb, w2_sb, w_in):
    with ExitStack() as st:
        def sb(name, shape, dt):
            return st.enter_context(nc.sbuf_tensor(name, shape, dt))

        def sem(name):
            return st.enter_context(nc.semaphore("e_" + name))

        tab = sb("tab", [P, E, 2], I32)
        b1_rows = sb("b1_rows", [P, E * FC // P, P], F32)
        b1T = sb("b1T", [P, E * FC], F32)
        b2p = sb("b2p", [PARTS, E * C], BF16)
        ones3 = sb("ones3", [PARTS, P], BF16)
        from_ids, to_ids = sb("from_ids", [P, U], I32), sb("to_ids", [P, U], I32)
        xg = sb("xg", [P, U, C], F32)
        xgT = sb("xgT", [P, 2, KC, P], F32)
        hT = sb("hT", [P, 2, FC, P], F32)
        h_hi, h_lo = sb("h_hi", [P, 2, FC, P], F32R), sb("h_lo", [P, 2, FC, P], F32R)
        w2_hi, w2_lo = sb("w2_hi", [P, 2, FC, C], F32R), sb("w2_lo", [P, 2, FC, C], F32R)
        yg = sb("yg", [P, U, C], F32)

        setup, tab_in, ones_ready = sem("setup"), sem("tab_in"), sem("ones")
        b1_psum, b1_ready = sem("b1_psum"), sem("b1_ready")
        ids_ready, to_ready = sem("ids"), sem("to_ready")
        gathered = [sem(f"gathered{r}") for r in range(U)]
        added, passed = sem("added"), sem("passed")
        xT_psum, xT_ready, h_psum, h_ready, y_psum, y_ready = (
            sem(n) for n in ("xT_psum", "xT_ready", "h_psum", "h_ready", "y_psum", "y_ready"))
        h_hi_ready, h_split, w2_hi_ready, w2_split = (sem(n) for n in ("h_hi_ready", "h_split", "w2_hi_ready", "w2_split"))
        blk = st.enter_context(nc.Block())

        @blk.sync
        def _(sp):
            sp.dma_start(tab[:].rearrange("p e t -> p (e t)"), tab_d.rearrange("(p e) t -> p (e t)", p=P)).then_inc(tab_in, 16)
            sp.dma_start(b1_rows[:], b1.rearrange("e (c p) -> (e c) p", p=P).rearrange("(g q) p -> q g p", q=P)).then_inc(setup, 16)
            sp.dma_start(b2p[:], bias_d[:, 0:E].rearrange("i e c -> i (e c)")).then_inc(setup, 16)

            def step(a):
                if a.exists and not (isinstance(a.s, int) and a.s <= U):
                    sp.wait_ge(y_psum, a.s - U)
                    load_expert(sp, w1, w2, w1_sb, w2_sb, w_in, a.b * U + a.u, a.u)

            steps(sp, E, 1, step)

        @blk.gpsimd
        def _(pool):
            pool.memset(ones3[:], 1.0).then_inc(ones_ready, 1)
            pool.wait_ge(tab_in, 16)

            def gather(a):
                wait(pool, xT_psum, a.s - U)
                wait_apart(pool, gathered[a.u], a.uses(4, 16), passed)
                pool.tensor_copy(from_ids[:, a.u:a.u + 1], tab[:, bass.ds(a.b * U + a.u, 1), 0]).then_inc(ids_ready, 1)
                wait_apart(pool, ids_ready, a.s, passed)
                pool.indirect_dma_start(out=xg[:, a.u], out_offset=None, in_=xn_d,
                                        in_offset=bass.IndirectOffsetOnAxis(ap=from_ids[:, a.u:a.u + 1].bitcast(U32), axis=0),
                                        bounds_check=N + P - 1).then_inc(gathered[a.u], 16)

            def add(a):
                wait_apart(pool, added, 16 * (a.s - 1), passed)
                pool.tensor_copy(to_ids[:, a.u:a.u + 1], tab[:, bass.ds(a.b * U + a.u, 1), 0]).then_inc(to_ready, 1)
                pool.wait_ge(to_ready, a.s)
                wait_apart(pool, y_ready, a.s, passed)
                pool.indirect_dma_start(out=out, out_offset=bass.IndirectOffsetOnAxis(ap=to_ids[:, a.u:a.u + 1].bitcast(U32), axis=0),
                                        in_=yg[:, a.u], in_offset=None, bounds_check=N + P - 1, compute_op=ALU.add
                                        ).then_inc(added, 16)

            def step(a):
                if a.back(-3).exists:
                    gather(a.back(-3))
                if a.back(1).exists:
                    add(a.back(1))

            for u in range(3):
                gather(At(0, u, E))
            steps(pool, E, 1, step)
            pool.wait_ge(added, 16 * E)

        @blk.tensor
        def _(pe):
            def tokens_by_channel(a):
                pe.wait_ge(gathered[a.u], a.uses(4, 16) + 16)
                wait(pe, xT_ready, a.s - 2)
                for c in range(KC):
                    mm = pe.transpose(ps[:, a.u % 2, c * P:(c + 1) * P], xg[:, a.u, c * P:(c + 1) * P], ident[:])
                mm.then_inc(xT_psum, 1)

            def first_layer(a):
                pe.wait_ge(w_in[a.u], a.uses(4, 32) + 32)
                pe.wait_ge(xT_ready, a.s)
                for n in range(FC):
                    if n % 4 == 0:
                        wait(pe, h_ready, FC * (a.s - 2))
                    for c in range(KC):
                        mm = pe.matmul(ps[:, 2 + 2 * (a.u % 2) + n // 4, (n % 4) * P:(n % 4 + 1) * P],
                                       w1_sb[:, a.u, c, n * P:(n + 1) * P], xgT[:, a.u % 2, c, :], start=(c == 0), stop=(c == KC - 1))
                    if n % 4 == 3:
                        mm.then_inc(h_psum, 1)

            def second_layer(a):
                pe.wait_ge(w2_split, a.s)
                wait(pe, y_ready, a.s - 2)
                bank = ps[:, 6 + a.u % 2, 0:C]
                pe.matmul(bank, ones3[:], b2p[:, bass.ds((a.b * U + a.u) * C, C)], start=True, stop=False)
                par = a.u % 2
                for n in range(FC):
                    if n % 4 == 0:
                        pe.wait_ge(h_split, 2 * (a.s - 1) + n // 4 + 1)
                    pe.matmul(bank, h_hi[:, par, n, :], w2_hi[:, par, n, :], start=False, stop=False)
                    pe.matmul(bank, h_hi[:, par, n, :], w2_lo[:, par, n, :], start=False, stop=False)
                    mm = pe.matmul(bank, h_lo[:, par, n, :], w2_hi[:, par, n, :], start=False, stop=(n == FC - 1))
                mm.then_inc(y_psum, 1)

            pe.wait_ge(setup, 32)
            pe.wait_ge(ones_ready, 1)
            for g in range(E * FC // P):
                mm = pe.transpose(ps[:, 7, g * P:(g + 1) * P], b1_rows[:, g, :], ident[:])
            mm.then_inc(b1_psum, 1)
            tokens_by_channel(At(0, 0, E))
            pe.wait_ge(b1_ready, 1)

            def step(a):
                if a.back(-1).exists:
                    tokens_by_channel(a.back(-1))
                if a.exists:
                    first_layer(a)
                if a.back(1).exists:
                    second_layer(a.back(1))

            steps(pe, E, 1, step)

        @blk.scalar
        def _(act):
            act.wait_ge(b1_psum, 1)
            act.copy(b1T[:], ps[:, 7, :]).then_inc(b1_ready, 1)
            act.wait_ge(b1_ready, 1)

            def step(a):
                if a.exists:
                    act.wait_ge(w_in[a.u], a.uses(4, 32) + 32)
                    wait(act, y_psum, a.s - 2)
                    act.copy(w2_hi[:, a.u % 2], w2_sb[:, a.u]).then_inc(w2_hi_ready, 1)
                    for n in range(FC):
                        if n % 4 == 0:
                            act.wait_ge(h_psum, FC // 4 * (a.s - 1) + n // 4 + 1)
                        act.activation(hT[:, a.u % 2, n, :], ps[:, 2 + 2 * (a.u % 2) + n // 4, (n % 4) * P:(n % 4 + 1) * P],
                                       ACT.Gelu, bias=b1T[:, bass.ds((a.b * U + a.u) * FC + n, 1)]).then_inc(h_ready, 1)
                        if n % 4 == 3:
                            act.wait_ge(h_ready, FC * (a.s - 1) + n + 1)
                            act.copy(h_hi[:, a.u % 2, n - 3:n + 1], hT[:, a.u % 2, n - 3:n + 1]).then_inc(h_hi_ready, 1)

            steps(act, E, 1, step)

        @blk.vector
        def _(dve):
            dve.wait_ge(tab_in, 16)

            def copy_tokens(a):
                dve.wait_ge(xT_psum, a.s)
                wait(dve, h_psum, FC // 4 * (a.s - 2))
                dve.tensor_copy(xgT[:, a.u % 2].rearrange("p c n -> p (c n)"), ps[:, a.u % 2, 0:C]).then_inc(xT_ready, 1)

            def scale_rows(a):
                dve.wait_ge(y_psum, a.s)
                wait(dve, added, 16 * (a.s - U))
                dve.tensor_scalar(yg[:, a.u], ps[:, 6 + a.u % 2, 0:C],
                                  tab[:, bass.ds(a.b * U + a.u, 1), 1].bitcast(F32), None, ALU.mult).then_inc(y_ready, 1)

            def second_parts(a):
                par = a.u % 2
                dve.wait_ge(w2_hi_ready, a.s)
                dve.tensor_tensor(w2_lo[:, par], w2_sb[:, a.u], w2_hi[:, par].bitcast(F32), ALU.subtract).then_inc(w2_split, 1)
                for half in range(2):
                    units = slice(half * FC // 2, (half + 1) * FC // 2)
                    dve.wait_ge(h_hi_ready, 2 * (a.s - 1) + half + 1)
                    dve.tensor_tensor(h_lo[:, par, units], hT[:, par, units], h_hi[:, par, units].bitcast(F32),
                                      ALU.subtract).then_inc(h_split, 1)

            copy_tokens(At(0, 0, E))

            def step(a):
                if a.back(-1).exists:
                    copy_tokens(a.back(-1))
                if a.exists:
                    second_parts(a)
                if a.back(1).exists:
                    scale_rows(a.back(1))

            steps(dve, E, 1, step)


_INS = ["x", "ctx_512", "L0_xattn_Wk", "L0_xattn_bk", "L0_xattn_Wq", "L0_xattn_bq", "L0_xattn_Wv", "L0_xattn_bv",
        "L0_xattn_Wck", "L0_xattn_bck", "L0_xattn_Wcq", "L0_xattn_bcq", "L0_xattn_Wcv", "L0_xattn_bcv",
        "L0_xattn_Wp", "L0_xattn_bp", "L0_ffn_gate_w", "L0_ffn_gate_b", "L0_ffn_w1", "L0_ffn_b1", "L0_ffn_w2", "L0_ffn_b2"]


def kernel(**inputs):
    import numpy as np
    import concourse.bacc as bacc
    from concourse.bass_utils import run_bass_kernel_spmd

    nc = bacc.Bacc("TRN2", target_bir_lowering=False, num_devices=1)
    arrays, args = {}, []
    for name in _INS:
        a = np.ascontiguousarray(inputs[name])
        arrays[f"in_{name}"] = a
        args.append(nc.dram_tensor(f"in_{name}", a.shape, mybir.dt.from_np(a.dtype), kind="ExternalInput").ap())
    out = nc.dram_tensor("out_rows", (N + P, C), F32, kind="ExternalOutput").ap()
    layer_kernel(nc, *args, out)
    r = run_bass_kernel_spmd(nc, [arrays], core_ids=[0])
    return r.results[0]["out_rows"][:N].reshape(B, S, C)
```
